# Optimizing a Trainium2 kernel written in Bass

```python
import numpy as np
import jax
import jax.numpy as jnp

def _softmax(x, axis=-1):
    return jax.nn.softmax(x, axis=axis)

def _gelu(x):
    return jax.nn.gelu(x, approximate=True)

def _silu(x):
    return jax.nn.silu(x)

def _sigmoid(x):
    return jax.nn.sigmoid(x)

def _layernorm(x, axis=-1, eps=1e-05):
    m = jnp.mean(x, axis=axis, keepdims=True)
    v = jnp.var(x, axis=axis, keepdims=True)
    return (x - m) / jnp.sqrt(v + eps)

def _scatter_add(tgt, idx, src, axis=0):
    return tgt.at[idx].add(src)

def _segment_sum(src, seg, n):
    return jax.ops.segment_sum(src, seg, n)
kernel_name = 'mk_xattn_ffn_d1_seqx_r8_11b690'

def setup_inputs(seed: int=0):
    np.random.seed(seed)
    _w = jnp.asarray

    def _rec_inputs():
        import jax
        import jax.numpy as jnp
        _rk = jax.random.key(seed)
        x = 0.0002417 + 0.9998 * jax.random.normal(jax.random.fold_in(_rk, 1), (64, 128, 128), jnp.float32)
        _lenS = 128 - jax.random.randint(jax.random.fold_in(_rk, 7), (64,), 0, max(1, 128 // 4) + 1, jnp.int32)
        _lenS2 = 77 - jax.random.randint(jax.random.fold_in(_rk, 8), (64,), 0, max(1, 77 // 4) + 1, jnp.int32)
        _ctx_1024P = jax.random.normal(jax.random.fold_in(_rk, 11), (64, 16, 128), jnp.float32)
        _ctx_1024c = jax.random.dirichlet(jax.random.fold_in(_rk, 511), 0.3 * jnp.ones((16,), jnp.float32), (64, 77))
        _ctx_1024t = jnp.einsum('bsk,bkd->bsd', _ctx_1024c, _ctx_1024P)
        _ctx_1024t = _ctx_1024t * jax.lax.rsqrt(jnp.mean(jnp.square(_ctx_1024t)) + 1e-12) * 0.953939
        ctx_1024 = 7.22013e-05 + 1.00017 * (_ctx_1024t + 0.3 * jax.random.normal(jax.random.fold_in(_rk, 611), (64, 77, 128), jnp.float32))
        return (x, ctx_1024)
    x, ctx_1024 = _rec_inputs()

    def _L0_xattn_setup():
        import jax, jax.numpy as jnp
        import numpy as np
        D_MODEL = 128
        B, S = (4, 256)
        key = jax.random.key(seed)
        ks = jax.random.split(key, 10)
        s = 1.0 / np.sqrt(D_MODEL)
        return {'k': jax.random.normal(ks[0], (B, S, D_MODEL), jnp.float32), 'v': jax.random.normal(ks[1], (B, S, D_MODEL), jnp.float32), 'q': jax.random.normal(ks[2], (B, S, D_MODEL), jnp.float32), 'Wk': jax.random.normal(ks[3], (D_MODEL, D_MODEL), jnp.float32) * s, 'Wv': jax.random.normal(ks[4], (D_MODEL, D_MODEL), jnp.float32) * s, 'bv': jnp.zeros((D_MODEL,), jnp.float32), 'Wq': jax.random.normal(ks[5], (D_MODEL, D_MODEL), jnp.float32) * s, 'bq': jnp.zeros((D_MODEL,), jnp.float32), 'Wo': jax.random.normal(ks[6], (D_MODEL, D_MODEL), jnp.float32) * s, 'bo': jnp.zeros((D_MODEL,), jnp.float32)}
    _L0_xattn_all = _L0_xattn_setup()
    _L0_xattn_in = {k: v for k, v in _L0_xattn_all.items() if k in ('Wk', 'Wv', 'bv', 'Wq', 'bq', 'Wo', 'bo')}
    del _L0_xattn_all

    def _L0_ffn_setup():
        import jax, jax.numpy as jnp
        import numpy as np
        HIDDEN = 128
        INTER = 512
        N_EXPERTS = 8

        def geglu(x, w1, w2, w3):
            return jax.nn.gelu(x @ w1, approximate=False) * (x @ w2) @ w3
        key = jax.random.key(seed)
        ks = jax.random.split(key, 8)
        s = 0.02
        x = jax.random.normal(ks[0], (2, 256, HIDDEN), dtype=jnp.float32)
        w1s = jax.random.normal(ks[1], (HIDDEN, INTER), dtype=jnp.float32) * s
        w2s = jax.random.normal(ks[2], (HIDDEN, INTER), dtype=jnp.float32) * s
        w3s = jax.random.normal(ks[3], (INTER, HIDDEN), dtype=jnp.float32) * s
        W1 = jax.random.normal(ks[4], (N_EXPERTS, HIDDEN, INTER), dtype=jnp.float32) * s
        W2 = jax.random.normal(ks[5], (N_EXPERTS, HIDDEN, INTER), dtype=jnp.float32) * s
        W3 = jax.random.normal(ks[6], (N_EXPERTS, INTER, HIDDEN), dtype=jnp.float32) * s
        Wg = jax.random.normal(ks[7], (HIDDEN, N_EXPERTS), dtype=jnp.float32) * s
        return {'x': x, 'w1s': w1s, 'w2s': w2s, 'w3s': w3s, 'W1': W1, 'W2': W2, 'W3': W3, 'Wg': Wg}
    _L0_ffn_all = _L0_ffn_setup()
    _L0_ffn_in = {k: v for k, v in _L0_ffn_all.items() if k in ('w1s', 'w2s', 'w3s', 'W1', 'W2', 'W3', 'Wg')}
    del _L0_ffn_all
    return {'x': x, 'ctx_1024': ctx_1024, 'L0_xattn_Wk': _L0_xattn_in['Wk'], 'L0_xattn_Wv': _L0_xattn_in['Wv'], 'L0_xattn_bv': _L0_xattn_in['bv'], 'L0_xattn_Wq': _L0_xattn_in['Wq'], 'L0_xattn_bq': _L0_xattn_in['bq'], 'L0_xattn_Wo': _L0_xattn_in['Wo'], 'L0_xattn_bo': _L0_xattn_in['bo'], 'L0_ffn_w1s': _L0_ffn_in['w1s'], 'L0_ffn_w2s': _L0_ffn_in['w2s'], 'L0_ffn_w3s': _L0_ffn_in['w3s'], 'L0_ffn_W1': _L0_ffn_in['W1'], 'L0_ffn_W2': _L0_ffn_in['W2'], 'L0_ffn_W3': _L0_ffn_in['W3'], 'L0_ffn_Wg': _L0_ffn_in['Wg']}

def reference(x, ctx_1024, L0_xattn_Wk, L0_xattn_Wv, L0_xattn_bv, L0_xattn_Wq, L0_xattn_bq, L0_xattn_Wo, L0_xattn_bo, L0_ffn_w1s, L0_ffn_w2s, L0_ffn_w3s, L0_ffn_W1, L0_ffn_W2, L0_ffn_W3, L0_ffn_Wg):
    import jax
    import jax.numpy as jnp

    def _L0_xattn_ref(k, v, q, Wk, Wv, bv, Wq, bq, Wo, bo):
        import jax, jax.numpy as jnp
        import numpy as np
        D_MODEL = 128
        B, S = (4, 256)
        kp = jnp.einsum('bsd,ed->bse', k, Wk)
        vp = jnp.einsum('bsd,ed->bse', v, Wv) + bv
        qp = jnp.einsum('bsd,ed->bse', q, Wq) + bq
        scale = 1.0 / jnp.sqrt(jnp.float32(kp.shape[-1]))
        scores = jnp.einsum('bqd,bkd->bqk', qp, kp) * scale
        probs = jax.nn.softmax(scores, axis=-1)
        ctx = jnp.einsum('bqk,bkd->bqd', probs, vp)
        return jnp.einsum('bqd,ed->bqe', ctx, Wo) + bo

    def _L0_ffn_ref(x, w1s, w2s, w3s, W1, W2, W3, Wg):
        import jax, jax.numpy as jnp
        import numpy as np
        HIDDEN = 128
        INTER = 512
        N_EXPERTS = 8

        def geglu(x, w1, w2, w3):
            return jax.nn.gelu(x @ w1, approximate=False) * (x @ w2) @ w3
        B, T, C = x.shape
        xf = x.reshape(-1, C)
        shared = geglu(xf, w1s, w2s, w3s)
        logits = xf @ Wg
        idx = jnp.argmax(logits, axis=-1)
        final = jnp.zeros_like(xf)
        for e in range(N_EXPERTS):
            y = geglu(xf, W1[e], W2[e], W3[e])
            final = final + jnp.where((idx == e)[:, None], y, 0.0)
        return (shared + final).reshape(B, T, C)
    x = x + _L0_xattn_ref(ctx_1024, ctx_1024, _layernorm(x, axis=-1), L0_xattn_Wk, L0_xattn_Wv, L0_xattn_bv, L0_xattn_Wq, L0_xattn_bq, L0_xattn_Wo, L0_xattn_bo)
    x = x + _L0_ffn_ref(_layernorm(x, axis=-1), L0_ffn_w1s, L0_ffn_w2s, L0_ffn_w3s, L0_ffn_W1, L0_ffn_W2, L0_ffn_W3, L0_ffn_Wg)
    return x

_drawn_inputs = setup_inputs


def setup_inputs(seed=0):
    import zlib

    import numpy as np

    out = dict(_drawn_inputs(seed))
    spreads = {'L0_xattn_bv': (0.0, 0.1), 'L0_xattn_bq': (0.0, 0.314), 'L0_xattn_bo': (0.0, 0.1)}
    factors = {'L0_ffn_w1s': 5.497,
     'L0_ffn_w2s': 5.373,
     'L0_ffn_w3s': 5.364,
     'L0_ffn_W1': 5.508,
     'L0_ffn_W2': 5.416,
     'L0_ffn_W3': 5.42,
     'L0_ffn_Wg': 5.775}
    for name, (base, spread) in spreads.items():
        noise = np.random.default_rng([zlib.crc32(name.encode()), seed]).standard_normal(out[name].shape)
        drawn = base * np.exp(spread * noise) if base else spread * noise
        out[name] = jnp.asarray(drawn.astype(out[name].dtype))
    for name, factor in factors.items():
        out[name] = (out[name] * factor).astype(out[name].dtype)
    return out
```

```python
from collections import namedtuple
from contextlib import ExitStack

import numpy as np
import concourse.bass as bass
from concourse import mybir

F32 = mybir.dt.float32
F32R = mybir.dt.float32r
BF16 = mybir.dt.bfloat16
I32 = mybir.dt.int32
ALU = mybir.AluOpType
ACT = mybir.ActivationFunctionType
AX = mybir.AxisListType

P = 128
B, K, D = 64, 77, 128
G = 4
NG = B // G
E, F = 8, 512
NK = F // P
TOK = B * P
TILES = (TOK + E * (P - 1)) // P
TCOL = TILES + 1
RING = 6
EPS = 1e-5
SCALE = 1.0 / float(np.sqrt(np.float32(D)))
NOWHERE = 4 * TOK

Step = namedtuple("Step", "n lap slot")


def step(h, off, ring):
    lap, slot = divmod(off, ring)
    return Step(h * ring + off, h + lap, slot)


def later_than(s, k):
    return not isinstance(s.n, int) or s.n >= k


def xattn_moe(nc, x, ctx_in, Wk, Wv, bv, Wq, bq, Wo, bo, w1s, w2s, w3s, W1, W2, W3, Wg, out):
    x_v = x.rearrange("b p d -> p b d")
    ctx_v = ctx_in.rearrange("b k d -> k b d")
    out_rows = out.rearrange("b p d -> (b p) d")
    rows = nc.dram_tensor("token_rows", (TOK, 2 * D), F32).ap()
    rows_v = rows.rearrange("(b p) c -> p b c", p=P)

    with ExitStack() as stack:
        def sb(name, shape, dt=F32):
            return stack.enter_context(nc.sbuf_tensor(name, shape, dt))

        def sem(name):
            return stack.enter_context(nc.semaphore(name))

        bank = [stack.enter_context(nc.psum_tensor(f"bank{i}", [P, 512], F32)) for i in range(8)]

        w12 = sb("w12", [P, (E + 1) * 4 * F], F32R)
        w3 = sb("w3", [P, (E + 1) * NK * D])
        wg = sb("wg", [P, E])
        ident = sb("ident", [P, P])
        neghalf = sb("neghalf", [P, G])
        bb = sb("bb", [P, D])
        fold_k = sb("fold_k", [P, P])
        fold_v = sb("fold_v", [P, P])
        fold_b = sb("fold_b", [P, P])
        res = sb("res", [P, B, D])
        n2T_all = sb("n2T_all", [P, TOK])
        at = [0]

        def over_n2T(cols, dt=F32):
            v = n2T_all[:, at[0]:at[0] + cols]
            at[0] += cols
            return v if dt == F32 else v.bitcast(dt)

        row_in = [over_n2T(2 * D) for _ in range(RING)]
        row_out = [over_n2T(D) for _ in range(RING)]
        ge = [over_n2T(F) for _ in range(2)]
        gg = [over_n2T(F) for _ in range(2)]
        gT = [over_n2T(F) for _ in range(2)]
        arena = sb("arena", [P, 6272])
        at2 = [0]

        def in_arena(cols):
            v = arena[:, at2[0]:at2[0] + cols]
            at2[0] += cols
            return v

        raw = [in_arena(F) for _ in range(2)]
        cx = [in_arena(G * D) for _ in range(2)]
        xn = [in_arena(G * D) for _ in range(2)]
        xnT = [in_arena(G * P) for _ in range(2)]
        cxT = [in_arena(G * K) for _ in range(2)]
        kt = [in_arena(G * K) for _ in range(2)]
        pr = [in_arena(G * K) for _ in range(2)]
        n2 = [sb(f"n2_{i}", [P, G * D]) for i in range(2)]
        tail = sb("tail", [P, G * (D + P)])
        vb, prT = tail[:, 0:G * D], tail[:, G * D:]
        tcmp = tail[0:1, 0:TCOL * E].rearrange("p (c e) -> p c e", e=E)
        te_f = tail[0:1, TCOL * E:TCOL * (E + 1)]
        own = tail[:, TCOL * (E + 1):TCOL * (E + 3)].rearrange("p (a c) -> p a c", a=2)
        at2[0] = 0
        n2T = sb("n2T", [P, G * P])
        sg = [in_arena(NK * 512) for _ in range(2)]
        sge = [in_arena(512) for _ in range(2)]
        cand = n2[0][:, :].rearrange("p (e b) -> p e b", e=E)
        cnt = n2[1][:, :]
        ohp = [in_arena(G * P // 2).bitcast(BF16).rearrange("p (g c) -> p g c", g=G) for _ in range(2)]
        ohc = [in_arena(G * TCOL).bitcast(BF16).rearrange("p (g a c) -> p g a c", g=G, a=2) for _ in range(2)]
        assert at2[0] <= 6272 and at[0] <= TOK
        shi = [sb(f"shi{i}", [P, 512], F32R) for i in range(2)]
        slo = [sb(f"slo{i}", [P, 512], F32R) for i in range(2)]
        xh = [shi[i][:, 0:P] for i in range(2)]
        xl = [slo[i][:, 0:P] for i in range(2)]
        wk_s, wq_s, wv_s, wo_s = (n2[0][:, i * P:(i + 1) * P] for i in range(4))
        woT = n2[1][:, 0:P]
        bq_r = n2[1][:, P:2 * P]
        bv_r = n2[1][:, 2 * P:3 * P]
        bo_r = n2[1][:, 3 * P:4 * P]
        bcol = sb("bcol", [P, 2])
        st1 = [sb(f"st1_{i}", [P, G, 6]) for i in range(2)]
        mv1 = [sb(f"mv1_{i}", [P, G, 2]) for i in range(2)]
        ve1 = [sb(f"ve1_{i}", [P, G]) for i in range(2)]
        rs1 = [sb(f"rs1_{i}", [P, G]) for i in range(2)]
        st2 = [sb(f"st2_{i}", [P, G, 6]) for i in range(2)]
        mv2 = [sb(f"mv2_{i}", [P, G, 2]) for i in range(2)]
        ve2 = [sb(f"ve2_{i}", [P, G]) for i in range(2)]
        rs2 = [sb(f"rs2_{i}", [P, G]) for i in range(2)]
        mx0 = sb("mx0", [P, G])
        nmx = [sb(f"nmx{i}", [P, G]) for i in range(2)]
        sm = [sb(f"sm{i}", [P, G]) for i in range(2)]
        rsm = sb("rsm", [P, G])
        lg = sb("lg", [P, E, B])
        oh = sb("oh", [P, E, B], BF16)
        iota_e = sb("iota_e", [P, E])
        best = sb("best", [P, B])
        tri = sb("tri", [P, P], BF16)
        ones_b = sb("ones_b", [P, P], BF16)
        ones_f = sb("ones_f", [P, 1])
        tot_i = sb("tot_i", [P, E], I32)
        ends = sb("ends", [P, E])
        tot = sb("tot", [P, E])
        tend = sb("tend", [P, E])
        shift = sb("shift", [P, E])
        pos_i = sb("pos_i", [P, B], I32)
        part_i = sb("part_i", [P, 2, B], I32)
        part = sb("part", [P, 2, B])
        iota_p = sb("iota_p", [P, P], BF16)
        iota_c = sb("iota_c", [P, TCOL], BF16)
        p1 = sb("p1", [P, 1])
        icol = sb("icol", [P, B])
        gid = sb("gid", [P, 2, TCOL], I32)
        te = sb("te", [1, TCOL], I32)
        gix = [sb(f"gix{i}", [P, 1], I32) for i in range(RING)]
        six = [sb(f"six{i}", [P, 1], I32) for i in range(RING)]

        names = """folds_loaded consts pool_consts dve_consts woT_ps woT_sb fold_ps fold_sb wshared_split
        w3_loaded wg_loaded half_split half_hi stats1 mv1_ready ve1_ready rstd1 xn_ready xnT_ps cxT_ps xnT_sb cxT_sb
        kt_ps v_ps kt_sb v_sb scores_ps max_ready nmax_ready exp_done rsum_ready probs_ready prT_ps prT_sb att_ps
        res_ready stats2 mv2_ready ve2_ready rstd2 n2_ready n2T_ps n2T_sb n2T_kept logits_ps logits_sb
        route onehot prefix_ps pos_ready te_ready hilo_hi hilo_ready up_ps gelu_done inner_ready down_ps acc_ready
        marks table_ps table_ready rows_stored
        idx_copied xT_ps x_hi x_ready r_up_ps r_gelu r_inner gT_ps gT_sb r_down_ps r_out dve_passed pool_passed""".split()
        S = {n: sem(n) for n in names}
        T = namedtuple("Sems", names)(**S)
        in_loaded = [sem(f"in_loaded{i}") for i in range(2)]
        raw_loaded = [sem(f"raw_loaded{i}") for i in range(2)]
        n2_stored = [sem(f"n2_stored{i}") for i in range(2)]
        acc_stored = [sem(f"acc_stored{i}") for i in range(2)]
        gathered = [sem(f"gathered{i}") for i in range(RING)]
        scattered = [sem(f"scattered{i}") for i in range(RING)]

        def b4(ap, w=D):
            return ap.rearrange("p (g d) -> p g d", g=G)

        def group(g):
            return bass.ds(g.n * G, G)

        def grp(h, off):
            return step(h, off, 2)

        def tile(h, off):
            return step(h, off, RING)

        def run_attention(eng, body, first, last):
            for i in range(0, first):
                body(grp(0, i), i)
            with eng.Fori(first // 2, last // 2) as h:
                for u in range(2):
                    body(grp(h, u), None)
            for i in range(last, NG + 2):
                body(grp(0, i), i)

        def ahead(g, k):
            lap, slot = divmod(g.slot + k, 2)
            return Step(g.n + k, g.lap + lap, slot)

        def has(i, k):
            return i is None or 0 <= i + k < NG

        def t_ahead(t, k):
            lap, slot = divmod(t.slot + k, RING)
            return Step(t.n + k, t.lap + lap, slot)

        def t_has(s, k):
            return s is None or 0 <= s + k < TILES

        def run_routed(eng, body):
            first = 3
            loops = (TILES - RING + 1 - first) // RING
            for s in range(-1, first):
                body(step(0, s, RING), s)
            with eng.Fori(0, loops) as h:
                for u in range(RING):
                    body(tile(h, first + u), None)
            for s in range(first + loops * RING, TILES + 1):
                body(tile(0, s), s)

        def carry(eng, passed):
            eng.sem_inc(passed, 1)

        block = stack.enter_context(nc.Block())

        @block.sync
        def _(sp):
            for dst, src in ((wk_s, Wk), (wq_s, Wq), (wv_s, Wv), (wo_s, Wo)):
                sp.dma_start(dst, src).then_inc(T.folds_loaded, 16)
            sp.dma_start(bcol[:, 0:1], bq.rearrange("(p o) -> p o", o=1)).then_inc(T.folds_loaded, 16)
            sp.dma_start(bcol[:, 1:2], bv.rearrange("(p o) -> p o", o=1)).then_inc(T.folds_loaded, 16)
            sp.dma_start(bo_r, bo.rearrange("(o d) -> o d", o=1).to_broadcast([P, D])).then_inc(T.folds_loaded, 16)

            def load_inputs(g):
                if later_than(g, 2):
                    sp.wait_ge(T.xn_ready, g.n - 1)
                    sp.wait_ge(T.cxT_ps, g.n - 1)
                sp.dma_start(res[:, group(g), :], x_v[:, group(g), :]).then_inc(in_loaded[g.slot], 16)
                sp.dma_start(b4(cx[g.slot])[0:K], ctx_v[:, group(g), :]).then_inc(in_loaded[g.slot], 16)

            def load_half(n):
                if later_than(n, 2):
                    sp.wait_ge(T.half_split, n.n - 1)
                src = (W1, W2)[n.slot]
                sp.dma_start(raw[n.slot], src[bass.ds(n.lap, 1), :, :].rearrange("e p f -> p (e f)")
                             ).then_inc(raw_loaded[n.slot], 16)

            load_inputs(grp(0, 0))
            load_inputs(grp(0, 1))
            for dst, src in ((0, w1s), (1, w2s)):
                sp.dma_start(tail[:, dst * F:(dst + 1) * F], src).then_inc(T.wshared_split, 16)
            sp.dma_start(wg[:, :], Wg).then_inc(T.wg_loaded, 16)
            sp.dma_start(w3[:, 0:E * NK * D].rearrange("p (s d) -> p s d", d=D),
                         W3.rearrange("e (k p) d -> p (e k) d", p=P)).then_inc(T.w3_loaded, 16)
            sp.dma_start(w3[:, E * NK * D:].rearrange("p (s d) -> p s d", d=D),
                         w3s.rearrange("(k p) d -> p k d", p=P)).then_inc(T.w3_loaded, 16)

            def body(g, i):
                if has(i, 2):
                    load_inputs(ahead(g, 2))
                if has(i, 0):
                    load_half(g)
                if has(i, -1):
                    c = ahead(g, -1)
                    sp.wait_ge(T.n2_ready, c.n + 1)
                    sp.dma_start(rows_v[:, group(c), D:2 * D], b4(n2[c.slot])).then_inc(n2_stored[c.slot], 16)

            run_attention(sp, body, 2, NG - 2)

            def store_acc(g):
                sp.wait_ge(T.acc_ready, g.n + 1)
                sp.dma_start(rows_v[:, group(g), 0:D], res[:, group(g), :]).then_inc(acc_stored[g.slot], 16)
            with sp.Fori(0, NG // 2) as h:
                for u in range(2):
                    store_acc(grp(h, u))
            for r in range(2):
                sp.wait_ge(acc_stored[r], 16 * (NG // 2))
                sp.wait_ge(n2_stored[r], 16 * (NG // 2))

        @block.gpsimd
        def _(pool):
            def const(ins):
                ins.then_inc(T.pool_consts, 1)
            const(nc.gpsimd.memset(ident[:, :], 0.0))
            const(nc.gpsimd.memset(ones_b[:, :], 1.0))
            const(nc.gpsimd.memset(neghalf[:, :], -0.5))
            const(nc.gpsimd.memset(ones_f[:, :], 1.0))
            const(nc.gpsimd.iota(iota_e[:, :], [[1, E]], base=0, channel_multiplier=0,
                                 allow_small_or_imprecise_dtypes=True))
            const(nc.gpsimd.iota(iota_p[:, :], [[1, P]], base=0, channel_multiplier=0,
                                 allow_small_or_imprecise_dtypes=True))
            const(nc.gpsimd.iota(iota_c[:, :], [[1, TCOL]], base=0, channel_multiplier=0,
                                 allow_small_or_imprecise_dtypes=True))
            const(nc.gpsimd.iota(p1[:, :], [[1, 1]], base=1, channel_multiplier=1,
                                 allow_small_or_imprecise_dtypes=True))
            const(nc.gpsimd.iota(icol[:, :], [[1, B]], base=0, channel_multiplier=0,
                                 allow_small_or_imprecise_dtypes=True))
            pool.wait_ge(T.pool_consts, 9)
            nc.gpsimd.affine_select(out=ident[:, :], in_=ident[:, :], compare_op=ALU.not_equal, fill=1.0, base=0,
                                    pattern=[[-1, P]], channel_multiplier=1).then_inc(T.consts, 1)
            nc.gpsimd.affine_select(out=tri[:, :], in_=ones_b[:, :], compare_op=ALU.is_gt, fill=0.0, base=0,
                                    pattern=[[1, P]], channel_multiplier=-1).then_inc(T.consts, 1)

            def split(raw_ap, base, hi_sem, lo_sem, n):
                hi = w12[:, bass.ds(base, F)]
                nc.gpsimd.tensor_copy(hi, raw_ap).then_inc(hi_sem, 1)
                pool.wait_ge(hi_sem, n)
                nc.gpsimd.tensor_tensor(w12[:, bass.ds(base + F, F)], raw_ap, hi.bitcast(F32), ALU.subtract
                                        ).then_inc(lo_sem, 1)

            def rstd(mv, ve, rs, g, mv_ready, ve_ready, rs_ready):
                pool.wait_ge(mv_ready, g.n + 1)
                carry(pool, T.pool_passed)
                nc.gpsimd.tensor_scalar(ve[g.slot][:, :], mv[g.slot][:, :, 1], EPS, None, ALU.add
                                        ).then_inc(ve_ready, 1)
                pool.wait_ge(ve_ready, g.n + 1)
                nc.gpsimd.tensor_tensor(rs[g.slot][:, :], ve[g.slot][:, :], neghalf[:, :], ALU.pow
                                        ).then_inc(rs_ready, 1)

            def body(g, i):
                if has(i, 1):
                    rstd(mv1, ve1, rs1, ahead(g, 1), T.mv1_ready, T.ve1_ready, T.rstd1)
                if has(i, 0):
                    pool.wait_ge(raw_loaded[g.slot], 16 * (g.lap + 1))
                    split(raw[g.slot], g.lap * 4 * F + g.slot * 2 * F, T.half_hi, T.half_split, g.n + 1)
                    rstd(mv2, ve2, rs2, g, T.mv2_ready, T.ve2_ready, T.rstd2)

            rstd(mv1, ve1, rs1, grp(0, 0), T.mv1_ready, T.ve1_ready, T.rstd1)
            run_attention(pool, body, 2, NG - 2)

            def slot(t, s):
                if t_has(s, -1):
                    o = t_ahead(t, -1)
                    pool.wait_ge(T.r_out, o.n + 1)
                    carry(pool, T.pool_passed)
                    nc.gpsimd.indirect_dma_start(
                        out_rows, bass.IndirectOffsetOnAxis(ap=six[o.slot][:, :], axis=0),
                        row_out[o.slot], None, bounds_check=TOK - 1, oob_is_err=False
                    ).then_inc(scattered[o.slot], 16)
                if t_has(s, RING - 1):
                    fetch(t_ahead(t, RING - 1))

            def fetch(t):
                if later_than(t, RING):
                    pool.wait_ge(scattered[t.slot], 16 * t.lap)
                nc.gpsimd.tensor_copy(gix[t.slot][:, :], gid[:, 0, bass.ds(t.n, 1)]).then_inc(T.idx_copied, 1)
                nc.gpsimd.tensor_copy(six[t.slot][:, :], gid[:, 1, bass.ds(t.n, 1)]).then_inc(T.idx_copied, 1)
                pool.wait_ge(T.idx_copied, 2 * t.n + 2)
                carry(pool, T.pool_passed)
                nc.gpsimd.indirect_dma_start(
                    row_in[t.slot], None, rows, bass.IndirectOffsetOnAxis(ap=gix[t.slot][:, :], axis=0),
                    bounds_check=TOK - 1, oob_is_err=False).then_inc(gathered[t.slot], 16)

            pool.wait_ge(T.table_ready, 1)
            pool.wait_ge(T.down_ps, NG)
            for r in range(2):
                pool.wait_ge(acc_stored[r], 16 * (NG // 2))
                pool.wait_ge(n2_stored[r], 16 * (NG // 2))
            for k in range(RING - 2):
                fetch(tile(0, k))
            run_routed(pool, slot)
            for r in range(RING):
                pool.wait_ge(scattered[r], 16 * ((TILES - r + RING - 1) // RING))

        @block.scalar
        def _(act):
            act.wait_ge(T.woT_ps, 1)
            nc.scalar.copy(woT, bank[0][:, 0:P]).then_inc(T.woT_sb, 1)

            def evac_in(g):
                act.wait_ge(T.xnT_ps, g.n + 1)
                if later_than(g, 2):
                    act.wait_ge(T.scores_ps, g.n - 1)
                nc.scalar.copy(xnT[g.slot], bank[0][:, :]).then_inc(T.xnT_sb, 1)
                act.wait_ge(T.cxT_ps, g.n + 1)
                nc.scalar.copy(cxT[g.slot], bank[1][:, 0:G * K]).then_inc(T.cxT_sb, 1)

            def body(g, i):
                if has(i, 0):
                    act.wait_ge(T.kt_ps, g.n + 1)
                    if later_than(g, 2):
                        act.wait_ge(T.scores_ps, g.n - 1)
                    nc.scalar.copy(kt[g.slot], bank[2][:, 0:G * K]).then_inc(T.kt_sb, 1)
                    act.wait_ge(T.nmax_ready, g.n + 1)
                    if later_than(g, 2):
                        act.wait_ge(T.prT_ps, g.n - 1)
                    for j in range(G):
                        last = nc.scalar.activation(pr[g.slot][:, j * K:(j + 1) * K], bank[4][:, j * K:(j + 1) * K],
                                                    ACT.Exp, bias=nmx[g.slot][:, j:j + 1], scale=SCALE,
                                                    accum_out=sm[g.slot][:, j:j + 1])
                    last.then_inc(T.exp_done, 1)
                if has(i, -1):
                    c = ahead(g, -1)
                    act.wait_ge(T.n2T_ps, c.n + 1)
                    if later_than(c, 1):
                        act.wait_ge(T.logits_ps, c.n)
                    nc.scalar.copy(n2T[:, :], bank[7][:, :]).then_inc(T.n2T_sb, 1)
                    nc.scalar.copy(n2T_all[:, bass.ds(c.n * 512, 512)], bank[7][:, :]).then_inc(T.n2T_kept, 1)
                if has(i, 1):
                    evac_in(ahead(g, 1))
                if has(i, 0):
                    act.wait_ge(T.prT_ps, g.n + 1)
                    if later_than(g, 1):
                        act.wait_ge(T.att_ps, g.n)
                    nc.scalar.copy(prT[0:K, :], bank[5][0:K, :]).then_inc(T.prT_sb, 1)

            evac_in(grp(0, 0))
            run_attention(act, body, 2, NG - 2)

            def gelu(g):
                for k in range(NK):
                    act.wait_ge(T.up_ps, NK * g.n + k + 1)
                    if k >= 2 or later_than(g, 1):
                        act.wait_ge(T.inner_ready, NK * g.n + k - 1)
                    nc.scalar.activation(sge[k % 2], bank[2 * (k % 2)][:, :], ACT.Gelu).then_inc(T.gelu_done, 1)

            act.wait_ge(T.att_ps, NG)
            gelu(grp(0, 0))
            with act.Fori(0, NG // 2 - 1) as h:
                gelu(grp(h, 1))
                gelu(grp(h, 2))
            gelu(grp(0, NG - 1))

            def slot(t, s):
                if t_has(s, -1):
                    o = t_ahead(t, -1)
                    act.wait_ge(T.gT_ps, o.n + 1)
                    if later_than(o, 2):
                        act.wait_ge(T.r_down_ps, o.n - 1)
                    nc.scalar.copy(gT[o.slot % 2], bank[4 + o.slot % 2][:, :]).then_inc(T.gT_sb, 1)
                if t_has(s, 1):
                    o = t_ahead(t, 1)
                    act.wait_ge(T.r_up_ps, o.n + 1)
                    if later_than(o, 2):
                        act.wait_ge(T.r_inner, o.n - 1)
                    nc.scalar.activation(ge[o.slot % 2], bank[2 * (o.slot % 2)][:, :], ACT.Gelu
                                         ).then_inc(T.r_gelu, 1)

            run_routed(act, slot)

        @block.vector
        def _(dve):
            dve.wait_ge(T.folds_loaded, 7 * 16)
            nc.vector.tensor_copy(bq_r, bcol[:, 0:1].to_broadcast([P, P])).then_inc(T.dve_consts, 1)
            nc.vector.tensor_copy(bv_r, bcol[:, 1:2].to_broadcast([P, P])).then_inc(T.dve_consts, 1)
            dve.wait_ge(T.fold_ps, 1)
            nc.vector.tensor_copy(fold_k[:, :], bank[1][:, 0:P]).then_inc(T.fold_sb, 1)
            nc.vector.tensor_copy(fold_b[:, :], bank[1][:, P:2 * P]).then_inc(T.fold_sb, 1)
            dve.wait_ge(T.fold_ps, 2)
            nc.vector.tensor_copy(fold_v[:, :], bank[2][:, 0:P]).then_inc(T.fold_sb, 1)
            nc.vector.tensor_tensor(bb[:, :], bank[2][:, P:2 * P], bo_r, ALU.add).then_inc(T.fold_sb, 1)
            dve.wait_ge(T.wshared_split, 32)
            for w in range(2):
                base = E * 4 * F + w * 2 * F
                nc.vector.tensor_copy(w12[:, base:base + F], tail[:, w * F:(w + 1) * F]).then_inc(T.hilo_hi, 1)
            dve.wait_ge(T.hilo_hi, 2)
            for w in range(2):
                base = E * 4 * F + w * 2 * F
                nc.vector.tensor_tensor(w12[:, base + F:base + 2 * F], tail[:, w * F:(w + 1) * F],
                                        w12[:, base:base + F].bitcast(F32), ALU.subtract).then_inc(T.dve_consts, 1)

            def norm_stats(src, st, mv, g, stats, ready):
                for j in range(G):
                    last = nc.vector.bn_stats(st[g.slot][:, j, :], src(j))
                last.then_inc(stats, 1)
                dve.wait_ge(stats, g.n + 1)
                carry(dve, T.dve_passed)
                for j in range(G):
                    last = nc.vector.bn_aggr(mv[g.slot][:, j, :], st[g.slot][:, j, :])
                last.then_inc(ready, 1)

            def batch(g, j):
                return res[:, bass.ds(g.n * G + j, 1), :].rearrange("p o d -> p (o d)")

            def stats1(g):
                dve.wait_ge(in_loaded[g.slot], 32 * (g.lap + 1))
                if later_than(g, 2):
                    dve.wait_ge(T.rstd1, g.n - 1)
                carry(dve, T.dve_passed)
                norm_stats(lambda j: batch(g, j), st1, mv1, g, T.stats1, T.mv1_ready)

            def normalise(dst, mv, rs, g, ready):
                for j in range(G):
                    last = nc.vector.tensor_scalar(b4(dst)[:, j, :], batch(g, j), mv[g.slot][:, j, 0:1],
                                                   rs[g.slot][:, j:j + 1], ALU.subtract, ALU.mult)
                last.then_inc(ready, 1)

            def norm1(g):
                dve.wait_ge(T.rstd1, g.n + 1)
                if later_than(g, 2):
                    dve.wait_ge(T.xnT_ps, g.n - 1)
                normalise(xn[g.slot], mv1, rs1, g, T.xn_ready)

            def body(g, i):
                if has(i, 0):
                    dve.wait_ge(T.v_ps, g.n + 1)
                    if later_than(g, 1):
                        dve.wait_ge(T.att_ps, g.n)
                    nc.vector.tensor_tensor(b4(vb[:, :])[0:K], b4(bank[3][:, :])[0:K],
                                            bb[0:K, :].unsqueeze(1).to_broadcast([K, G, D]), ALU.add
                                            ).then_inc(T.v_sb, 1)
                    dve.wait_ge(T.scores_ps, g.n + 1)
                    nc.vector.reduce_max(mx0[:, :], bank[4][:, 0:G * K].rearrange("p (g k) -> p g k", g=G),
                                         AX.X).then_inc(T.max_ready, 1)
                    if later_than(g, 2):
                        dve.wait_ge(T.exp_done, g.n - 1)
                    dve.wait_ge(T.max_ready, g.n + 1)
                    nc.vector.tensor_scalar(nmx[g.slot][:, :], mx0[:, :], -SCALE, None, ALU.mult
                                            ).then_inc(T.nmax_ready, 1)
                if has(i, -1):
                    c = ahead(g, -1)
                    dve.wait_ge(T.rstd2, c.n + 1)
                    if later_than(c, 2):
                        dve.wait_ge(T.n2T_ps, c.n - 1)
                        dve.wait_ge(n2_stored[c.slot], 16 * c.lap)
                    normalise(n2[c.slot][:, :], mv2, rs2, c, T.n2_ready)
                if has(i, 1):
                    stats1(ahead(g, 1))
                    norm1(ahead(g, 1))
                if has(i, -1):
                    c = ahead(g, -1)
                    dve.wait_ge(T.logits_ps, c.n + 1)
                    nc.vector.tensor_copy(lg[:, :, group(c)],
                                          bank[2][:, 320:320 + G * E].rearrange("p (g e) -> p e g", g=G)
                                          ).then_inc(T.logits_sb, 1)
                if has(i, 0):
                    dve.wait_ge(T.exp_done, g.n + 1)
                    nc.vector.reciprocal(rsm[:, :], sm[g.slot][:, :]).then_inc(T.rsum_ready, 1)
                    dve.wait_ge(T.rsum_ready, g.n + 1)
                    pv = pr[g.slot].rearrange("p (g k) -> p g k", g=G)
                    nc.vector.tensor_tensor(pv, pv, rsm[:, :].unsqueeze(2).to_broadcast([P, G, K]), ALU.mult
                                            ).then_inc(T.probs_ready, 1)
                    dve.wait_ge(T.att_ps, g.n + 1)
                    nc.vector.tensor_tensor(res[:, group(g), :], res[:, group(g), :], b4(bank[6][:, :]), ALU.add
                                            ).then_inc(T.res_ready, 1)
                    dve.wait_ge(T.res_ready, g.n + 1)
                    if later_than(g, 2):
                        dve.wait_ge(T.rstd2, g.n - 1)
                    carry(dve, T.dve_passed)
                    norm_stats(lambda j: batch(g, j), st2, mv2, g, T.stats2, T.mv2_ready)

            stats1(grp(0, 0))
            dve.wait_ge(T.fold_sb, 4)
            norm1(grp(0, 0))
            run_attention(dve, body, 2, NG - 2)

            def hilo(g):
                if later_than(g, 2):
                    dve.wait_ge(T.up_ps, NK * (g.n - 1))
                src = n2T_all[:, bass.ds(g.n * 512, 512)]
                nc.vector.tensor_copy(shi[g.slot][:, :], src).then_inc(T.hilo_hi, 1)
                dve.wait_ge(T.hilo_hi, g.n + 3)
                nc.vector.tensor_tensor(slo[g.slot][:, :], src, shi[g.slot][:, :].bitcast(F32), ALU.subtract
                                        ).then_inc(T.hilo_ready, 1)

            def inner(g):
                for k in range(NK):
                    dve.wait_ge(T.gelu_done, NK * g.n + k + 1)
                    if k == 0 and later_than(g, 2):
                        dve.wait_ge(T.down_ps, g.n - 1)
                    nc.vector.tensor_tensor(sg[g.slot][:, k * 512:(k + 1) * 512], sge[k % 2],
                                            bank[2 * (k % 2) + 1][:, :], ALU.mult).then_inc(T.inner_ready, 1)

            def mark(g):
                if later_than(g, 2):
                    dve.wait_ge(T.table_ps, g.n - 1)
                for j in range(G):
                    i = bass.ds(g.n * G + j, 1)
                    nc.vector.tensor_scalar(ohp[g.slot][:, j, :], iota_p[:, :], part[:, 1, i], None, ALU.is_equal)
                    nc.vector.tensor_scalar(ohc[g.slot][:, j, 0, :], iota_c[:, :], part[:, 0, i], p1[:, :],
                                            ALU.is_equal, ALU.mult)
                    last = nc.vector.tensor_scalar(ohc[g.slot][:, j, 1, :], iota_c[:, :], part[:, 0, i],
                                                   icol[:, i], ALU.is_equal, ALU.mult)
                last.then_inc(T.marks, 1)

            def accumulate(g):
                dve.wait_ge(T.down_ps, g.n + 1)
                nc.vector.tensor_tensor(res[:, group(g), :], res[:, group(g), :], b4(bank[4][:, :]), ALU.add
                                        ).then_inc(T.acc_ready, 1)

            links = [0]

            def link(ins):
                links[0] += 1
                ins.then_inc(T.route, 1)
                dve.wait_ge(T.route, links[0])

            def by_tile(ap):
                return ap.rearrange("p e b -> p b e")

            dve.wait_ge(T.n2T_kept, NG)
            hilo(grp(0, 0))
            dve.wait_ge(T.logits_sb, NG)
            for q in range(2):
                dve.wait_ge(n2_stored[q], 16 * (NG // 2))
            link(nc.vector.reduce_max(best[:, :], by_tile(lg[:, :, :]), AX.X))
            link(nc.vector.tensor_tensor(lg[:, :, :], lg[:, :, :], best[:, :].unsqueeze(1).to_broadcast([P, E, B]),
                                         ALU.is_equal))
            link(nc.vector.tensor_scalar(lg[:, :, :], lg[:, :, :], -float(E), None, ALU.mult))
            link(nc.vector.tensor_tensor(cand[:, :, :], lg[:, :, :], iota_e[:, :].unsqueeze(2).to_broadcast([P, E, B]), ALU.add))
            link(nc.vector.tensor_reduce(best[:, :], by_tile(cand[:, :, :]), AX.X, ALU.min))
            nc.vector.tensor_tensor(oh[:, :, :], cand[:, :, :], best[:, :].unsqueeze(1).to_broadcast([P, E, B]),
                                    ALU.is_equal).then_inc(T.onehot, 1)
            inner(grp(0, 0))
            hilo(grp(0, 1))
            dve.wait_ge(T.prefix_ps, 1)
            link(nc.vector.tensor_tensor_scan(cnt[:, :], ones_f[:, :].to_broadcast([P, E * B]), bank[6][:, :], 0.0, ALU.mult, ALU.add))
            cnt3 = cnt[:, :].rearrange("p (e b) -> p e b", e=E)
            link(nc.vector.tensor_copy(ends[:, :], cnt3[:, :, B - 1]))
            link(nc.vector.tensor_copy(tot[:, :], ends[:, :]))
            link(nc.vector.tensor_tensor(tot[:, 1:E], ends[:, 1:E], ends[:, 0:E - 1], ALU.subtract))
            link(nc.vector.tensor_scalar(tot_i[:, :], tot[:, :], float(P - 1), None, ALU.add))
            link(nc.vector.tensor_single_scalar(tot_i[:, :], tot_i[:, :], 7, ALU.arith_shift_right))
            link(nc.vector.tensor_copy(tot[:, :], tot_i[:, :]))
            link(nc.vector.tensor_tensor_scan(tend[:, :], ones_f[:, :].to_broadcast([P, E]), tot[:, :], 0.0, ALU.mult, ALU.add))
            link(nc.vector.memset(shift[:, 0:1], 0.0))
            link(nc.vector.tensor_scalar(shift[:, 1:E], tend[:, 0:E - 1], float(P), None, ALU.mult))
            link(nc.vector.tensor_tensor(shift[:, 1:E], shift[:, 1:E], ends[:, 0:E - 1], ALU.subtract))
            link(nc.vector.tensor_tensor(cnt[:, :], cnt[:, :], bank[6][:, :], ALU.subtract))
            link(nc.vector.tensor_tensor(cnt[:, :], cnt[:, :], bank[7][:, :], ALU.add))
            link(nc.vector.tensor_tensor(cnt3, cnt3, shift[:, :].unsqueeze(2).to_broadcast([P, E, B]), ALU.add))
            link(nc.vector.tensor_tensor(cnt3, cnt3, oh[:, :, :], ALU.mult))
            link(nc.vector.tensor_reduce(best[:, :], by_tile(cnt3), AX.X, ALU.add))
            link(nc.vector.tensor_copy(pos_i[:, :], best[:, :]))
            link(nc.vector.tensor_single_scalar(part_i[:, 0, :], pos_i[:, :], 7, ALU.arith_shift_right))
            link(nc.vector.tensor_single_scalar(part_i[:, 1, :], pos_i[:, :], P - 1, ALU.bitwise_and))
            link(nc.vector.tensor_copy(part[:, :, :], part_i[:, :, :]))
            link(nc.vector.tensor_tensor(tcmp[:, :, :], iota_c[0:1, :].unsqueeze(2).to_broadcast([1, TCOL, E]),
                                         tend[0:1, :].unsqueeze(1).to_broadcast([1, TCOL, E]), ALU.is_ge))
            link(nc.vector.tensor_reduce(te_f[:, :], tcmp[:, :, :], AX.X, ALU.add))
            link(nc.vector.tensor_scalar(te[:, :], te_f[:, :], float(E - 1), None, ALU.min))

            def shared_body(g, last=False):
                inner(g)
                if not last:
                    hilo(ahead(g, 1))
                mark(ahead(g, -1))
                accumulate(ahead(g, -1))

            shared_body(grp(0, 1))
            shared_body(grp(0, 2))
            with dve.Fori(1, NG // 2 - 1) as h:
                shared_body(grp(h, 1))
                shared_body(grp(h, 2))
            shared_body(grp(0, NG - 1), last=True)
            mark(grp(0, NG - 1))
            accumulate(grp(0, NG - 1))
            dve.wait_ge(T.table_ps, NG)
            tb = bank[5][:, 0:2 * TCOL].rearrange("p (a c) -> p a c", a=2)
            link(nc.vector.tensor_scalar(own[:, 0, :], tb[:, 1, :], float(P), -1.0, ALU.mult, ALU.add))
            link(nc.vector.tensor_tensor(own[:, 0, :], own[:, 0, :], tb[:, 0, :], ALU.add))
            link(nc.vector.tensor_scalar(own[:, 1, :], own[:, 0, :], 0.0, float(NOWHERE), ALU.is_lt, ALU.mult))
            link(nc.vector.tensor_scalar(own[:, 0, :], own[:, 0, :], 0.0, None, ALU.max))
            link(nc.vector.tensor_tensor(own[:, 1, :], own[:, 1, :], own[:, 0, :], ALU.add))
            nc.vector.tensor_copy(gid[:, :, :], own[:, :, :]).then_inc(T.table_ready, 1)

            def slot(t, s):
                if t_has(s, 2):
                    parts(t_ahead(t, 2))
                if t_has(s, 1):
                    o = t_ahead(t, 1)
                    dve.wait_ge(T.r_gelu, o.n + 1)
                    if later_than(o, 2):
                        dve.wait_ge(T.gT_ps, o.n - 1)
                    nc.vector.tensor_tensor(gg[o.slot % 2], ge[o.slot % 2], bank[2 * (o.slot % 2) + 1][:, :],
                                            ALU.mult).then_inc(T.r_inner, 1)
                if t_has(s, -1):
                    o = t_ahead(t, -1)
                    dve.wait_ge(T.r_down_ps, o.n + 1)
                    if later_than(o, RING):
                        dve.wait_ge(scattered[o.slot], 16 * o.lap)
                    nc.vector.tensor_tensor(row_out[o.slot], row_in[o.slot][:, 0:D],
                                            bank[6][:, 0:P], ALU.add
                                            ).then_inc(T.r_out, 1)

            def parts(t):
                dve.wait_ge(T.xT_ps, t.n + 1)
                if later_than(t, 2):
                    dve.wait_ge(T.r_up_ps, t.n - 1)
                src = bank[7][:, 0:P]
                nc.vector.tensor_copy(xh[t.slot % 2], src).then_inc(T.x_hi, 1)
                dve.wait_ge(T.x_hi, t.n + 1)
                nc.vector.tensor_tensor(xl[t.slot % 2], src, xh[t.slot % 2].bitcast(F32), ALU.subtract
                                        ).then_inc(T.x_ready, 1)

            parts(tile(0, 0))
            run_routed(dve, slot)

        @block.tensor
        def _(pe):
            mm, tr = nc.tensor.matmul, nc.tensor.transpose
            pe.wait_ge(T.consts, 2)
            pe.wait_ge(T.folds_loaded, 7 * 16)
            tr(bank[0][:, 0:P], wo_s, ident[:, :]).then_inc(T.woT_ps, 1)
            pe.wait_ge(T.dve_consts, 2)
            mm(bank[1][:, 0:P], wk_s, wq_s, start=True, stop=True)
            mm(bank[1][:, P:2 * P], wk_s, bq_r, start=True, stop=True).then_inc(T.fold_ps, 1)
            pe.wait_ge(T.woT_sb, 1)
            mm(bank[2][:, 0:P], wv_s, woT, start=True, stop=True)
            mm(bank[2][:, P:2 * P], bv_r, woT, start=True, stop=True).then_inc(T.fold_ps, 1)
            pe.wait_ge(T.fold_sb, 4)

            def transpose_in(g):
                pe.wait_ge(T.xn_ready, g.n + 1)
                if later_than(g, 1):
                    pe.wait_ge(T.xnT_sb, g.n)
                for j in range(G):
                    last = tr(bank[0][:, j * P:(j + 1) * P], b4(xn[g.slot])[:, j, :], ident[:, :])
                last.then_inc(T.xnT_ps, 1)
                pe.wait_ge(in_loaded[g.slot], 32 * (g.lap + 1))
                if later_than(g, 1):
                    pe.wait_ge(T.cxT_sb, g.n)
                for j in range(G):
                    last = tr(bank[1][:, j * K:(j + 1) * K], b4(cx[g.slot])[0:K, j, :], ident[0:K, 0:K])
                last.then_inc(T.cxT_ps, 1)

            def project(g):
                pe.wait_ge(T.cxT_sb, g.n + 1)
                if later_than(g, 1):
                    pe.wait_ge(T.kt_sb, g.n)
                mm(bank[2][:, 0:G * K], fold_k[:, :], cxT[g.slot], start=True, stop=True).then_inc(T.kt_ps, 1)
                if later_than(g, 1):
                    pe.wait_ge(T.v_sb, g.n)
                for j in range(G):
                    last = mm(bank[3][0:K, j * D:(j + 1) * D], cxT[g.slot][:, j * K:(j + 1) * K], fold_v[:, :],
                              start=True, stop=True)
                last.then_inc(T.v_ps, 1)

            def scores(g):
                pe.wait_ge(T.kt_sb, g.n + 1)
                pe.wait_ge(T.xnT_sb, g.n + 1)
                if later_than(g, 1):
                    pe.wait_ge(T.exp_done, g.n)
                for j in range(G):
                    mm(bank[4][:, j * K:(j + 1) * K], fold_b[:, :], cxT[g.slot][:, j * K:(j + 1) * K],
                       start=True, stop=False)
                    last = mm(bank[4][:, j * K:(j + 1) * K], xnT[g.slot][:, j * P:(j + 1) * P],
                              kt[g.slot][:, j * K:(j + 1) * K], start=False, stop=True)
                last.then_inc(T.scores_ps, 1)

            def attend(g):
                pe.wait_ge(T.probs_ready, g.n + 1)
                if later_than(g, 1):
                    pe.wait_ge(T.prT_sb, g.n)
                for j in range(G):
                    last = tr(bank[5][0:K, j * P:(j + 1) * P], pr[g.slot][:, j * K:(j + 1) * K], ident[:, :])
                last.then_inc(T.prT_ps, 1)
                pe.wait_ge(T.prT_sb, g.n + 1)
                pe.wait_ge(T.v_sb, g.n + 1)
                if later_than(g, 1):
                    pe.wait_ge(T.res_ready, g.n)
                for j in range(G):
                    last = mm(bank[6][:, j * D:(j + 1) * D], prT[0:K, j * P:(j + 1) * P],
                              vb[0:K, j * D:(j + 1) * D], start=True, stop=True)
                last.then_inc(T.att_ps, 1)

            def body(g, i):
                if has(i, 0):
                    project(g)
                    scores(g)
                if has(i, -1):
                    c = ahead(g, -1)
                    pe.wait_ge(T.n2_ready, c.n + 1)
                    if later_than(c, 1):
                        pe.wait_ge(T.n2T_kept, c.n)
                    for j in range(G):
                        last = tr(bank[7][:, j * P:(j + 1) * P], n2[c.slot][:, j * D:(j + 1) * D], ident[:, :])
                    last.then_inc(T.n2T_ps, 1)
                if has(i, 1):
                    transpose_in(ahead(g, 1))
                if has(i, -1):
                    pe.wait_ge(T.n2T_sb, c.n + 1)
                    if later_than(c, 1):
                        pe.wait_ge(T.logits_sb, c.n)
                    if has(i, 0):
                        pe.wait_ge(T.kt_sb, g.n + 1)
                    for j in range(G):
                        last = mm(bank[2][:, 320 + j * E:320 + (j + 1) * E], n2T[:, j * P:(j + 1) * P], wg[:, :],
                                  start=True, stop=True)
                    last.then_inc(T.logits_ps, 1)
                if has(i, 0):
                    attend(g)

            transpose_in(grp(0, 0))
            pe.wait_ge(T.wg_loaded, 16)
            run_attention(pe, body, 2, NG - 2)

            def up(g):
                pe.wait_ge(T.hilo_ready, g.n + 1)
                for k in range(NK):
                    if k >= 2 or later_than(g, 1):
                        pe.wait_ge(T.inner_ready, NK * g.n + k - 1)
                    for w in range(2):
                        base = E * 4 * F + w * 2 * F + k * P
                        hi, lo = w12[:, base:base + P], w12[:, base + F:base + F + P]
                        dst = bank[2 * (k % 2) + w][:, :]
                        mm(dst, hi, shi[g.slot][:, :], start=True, stop=False)
                        mm(dst, hi, slo[g.slot][:, :], start=False, stop=False)
                        last = mm(dst, lo, shi[g.slot][:, :], start=False, stop=True)
                    last.then_inc(T.up_ps, 1)

            def down(g):
                pe.wait_ge(T.inner_ready, NK * (g.n + 1))
                if later_than(g, 1):
                    pe.wait_ge(T.acc_ready, g.n)
                for j in range(G):
                    for k in range(NK):
                        last = mm(bank[4][:, j * D:(j + 1) * D], sg[g.slot][:, k * 512 + j * P:k * 512 + (j + 1) * P],
                                  w3[:, (E * NK + k) * D:(E * NK + k + 1) * D], start=k == 0, stop=k == NK - 1)
                last.then_inc(T.down_ps, 1)

            def table(g, first=False, final=False):
                pe.wait_ge(T.marks, g.n + 1)
                for j in range(G):
                    last = mm(bank[5][:, 0:2 * TCOL], ohp[g.slot][:, j, :],
                              ohc[g.slot][:, j, :, :].rearrange("p a c -> p (a c)"),
                              start=first and j == 0, stop=final and j == G - 1)
                last.then_inc(T.table_ps, 1)

            def shared_body(g, first=False):
                up(g)
                down(ahead(g, -1))
                table(ahead(g, -1), first=first)

            pe.wait_ge(T.w3_loaded, 32)
            pe.wait_ge(T.dve_consts, 4)
            pe.wait_ge(T.exp_done, NG)
            up(grp(0, 0))
            pe.wait_ge(T.onehot, 1)
            oh_f = oh[:, :, :].rearrange("p e b -> p (e b)")
            mm(bank[6][:, :], ones_b[:, :], oh_f, start=True, stop=True)
            mm(bank[7][:, :], tri[:, :], oh_f, start=True, stop=True).then_inc(T.prefix_ps, 1)
            shared_body(grp(0, 1), first=True)
            shared_body(grp(0, 2))
            with pe.Fori(1, NG // 2 - 1) as h:
                shared_body(grp(h, 1))
                shared_body(grp(h, 2))
            shared_body(grp(0, NG - 1))
            down(grp(0, NG - 1))
            table(grp(0, NG - 1), final=True)

            def fetch_T(t):
                pe.wait_ge(gathered[t.slot], 16 * (t.lap + 1))
                if later_than(t, 1):
                    pe.wait_ge(T.x_ready, t.n)
                tr(bank[7][:, 0:P], row_in[t.slot][:, D:2 * D], ident[:, :]
                   ).then_inc(T.xT_ps, 1)

            def r_up(t):
                e = pe.value_load(te[0:1, bass.ds(t.n, 1)], min_val=0, max_val=E - 1)
                pe.wait_ge(T.x_ready, t.n + 1)
                if later_than(t, 2):
                    pe.wait_ge(T.r_inner, t.n - 1)
                q = t.slot % 2
                for w in range(2):
                    hi = w12[:, bass.ds(e * (4 * F) + w * 2 * F, F)]
                    lo = w12[:, bass.ds(e * (4 * F) + w * 2 * F + F, F)]
                    dst = bank[2 * q + w][:, :]
                    mm(dst, xh[q], hi, start=True, stop=False)
                    mm(dst, xh[q], lo, start=False, stop=False)
                    last = mm(dst, xl[q], hi, start=False, stop=True)
                last.then_inc(T.r_up_ps, 1)

            def slot(t, s):
                if t_has(s, -1):
                    o = t_ahead(t, -1)
                    pe.wait_ge(T.r_inner, o.n + 1)
                    if later_than(o, 2):
                        pe.wait_ge(T.gT_sb, o.n - 1)
                    for k in range(NK):
                        last = tr(bank[4 + o.slot % 2][:, k * P:(k + 1) * P], gg[o.slot % 2][:, k * P:(k + 1) * P],
                                  ident[:, :])
                    last.then_inc(T.gT_ps, 1)
                if t_has(s, 2):
                    fetch_T(t_ahead(t, 2))
                if t_has(s, 1):
                    r_up(t_ahead(t, 1))
                if t_has(s, -1):
                    e = pe.value_load(te[0:1, bass.ds(o.n, 1)], min_val=0, max_val=E - 1)
                    pe.wait_ge(T.gT_sb, o.n + 1)
                    if later_than(o, 1):
                        pe.wait_ge(T.r_out, o.n)
                    for k in range(NK):
                        last = mm(bank[6][:, 0:P],
                                  gT[o.slot % 2][:, k * P:(k + 1) * P],
                                  w3[:, bass.ds(e * (NK * D) + k * D, D)], start=k == 0, stop=k == NK - 1)
                    last.then_inc(T.r_down_ps, 1)

            pe.wait_ge(T.table_ready, 1)
            pe.wait_ge(T.half_split, NG)
            fetch_T(tile(0, 0))
            run_routed(pe, slot)


_INS = ['x', 'ctx_1024', 'L0_xattn_Wk', 'L0_xattn_Wv', 'L0_xattn_bv', 'L0_xattn_Wq', 'L0_xattn_bq', 'L0_xattn_Wo',
        'L0_xattn_bo', 'L0_ffn_w1s', 'L0_ffn_w2s', 'L0_ffn_w3s', 'L0_ffn_W1', 'L0_ffn_W2', 'L0_ffn_W3', 'L0_ffn_Wg']


def kernel(**inputs):
    import concourse.bacc as bacc
    from concourse.bass_utils import run_bass_kernel_spmd

    nc = bacc.Bacc("TRN2", target_bir_lowering=False, num_devices=1)
    arrays, args = {}, []
    for name in _INS:
        a = np.ascontiguousarray(inputs[name])
        arrays[name] = a
        args.append(nc.dram_tensor(name, a.shape, mybir.dt.from_np(a.dtype), kind="ExternalInput").ap())
    args.append(nc.dram_tensor("y", (B, P, D), F32, kind="ExternalOutput").ap())
    xattn_moe(nc, *args)
    r = run_bass_kernel_spmd(nc, [arrays], core_ids=[0])
    return r.results[0]["y"]
```

```python
from collections import namedtuple
from contextlib import ExitStack

import numpy as np
import concourse.bass as bass
from concourse import mybir

F32 = mybir.dt.float32
F32R = mybir.dt.float32r
BF16 = mybir.dt.bfloat16
I32 = mybir.dt.int32
ALU = mybir.AluOpType
ACT = mybir.ActivationFunctionType
AX = mybir.AxisListType

P = 128
B, K, D = 64, 77, 128
G = 4
NG = B // G
E, F = 8, 512
NK = F // P
TOK = B * P
TILES = (TOK + E * (P - 1)) // P
TCOL = TILES + 1
RING = 6
EPS = 1e-5
SCALE = 1.0 / float(np.sqrt(np.float32(D)))
NOWHERE = 4 * TOK

Step = namedtuple("Step", "n lap slot")


def step(h, off, ring):
    lap, slot = divmod(off, ring)
    return Step(h * ring + off, h + lap, slot)


def later_than(s, k):
    return not isinstance(s.n, int) or s.n >= k


def xattn_moe(nc, x, ctx_in, Wk, Wv, bv, Wq, bq, Wo, bo, w1s, w2s, w3s, W1, W2, W3, Wg, out):
    x_v = x.rearrange("b p d -> p b d")
    ctx_v = ctx_in.rearrange("b k d -> k b d")
    out_rows = out.rearrange("b p d -> (b p) d")
    rows = nc.dram_tensor("token_rows", (TOK, 2 * D), F32).ap()
    rows_v = rows.rearrange("(b p) c -> p b c", p=P)

    with ExitStack() as stack:
        def sb(name, shape, dt=F32):
            return stack.enter_context(nc.sbuf_tensor(name, shape, dt))

        def sem(name):
            return stack.enter_context(nc.semaphore(name))

        bank = [stack.enter_context(nc.psum_tensor(f"bank{i}", [P, 512], F32)) for i in range(8)]

        w12 = sb("w12", [P, (E + 1) * 4 * F], F32R)
        w3 = sb("w3", [P, (E + 1) * NK * D])
        wg = sb("wg", [P, E])
        ident = sb("ident", [P, P])
        neghalf = sb("neghalf", [P, G])
        bb = sb("bb", [P, D])
        fold_q = sb("fold_q", [P, P])
        fold_v = sb("fold_v", [P, P])
        q_bias = sb("q_bias", [P, 1])
        res = sb("res", [P, B, D])
        raw = [sb(f"raw{i}", [P, F]) for i in range(2)]
        cx = [sb(f"cx{i}", [P, G * D]) for i in range(2)]
        xn = sb("xn", [P, G * D])
        xnT = sb("xnT", [P, G * P])
        cxT = sb("cxT", [P, G * K])
        qT = sb("qT", [P, G * P])
        pr = sb("pr", [P, G * K])
        prT = sb("prT", [P, G * P])
        vb = sb("vb", [P, G * D])
        n2 = [sb(f"n2_{i}", [P, G * D]) for i in range(2)]
        n2T = sb("n2T", [P, G * P])
        shi = [sb(f"shi{i}", [P, G * P], F32R) for i in range(2)]
        slo = [sb(f"slo{i}", [P, G * P], F32R) for i in range(2)]
        sg = [sb(f"sg{i}", [P, NK * G * P]) for i in range(2)]
        sge = sb("sge", [P, G * P])
        row_in = [sb(f"row_in{i}", [P, 2 * D])[:, :] for i in range(RING)]
        row_out = [sb(f"row_out{i}", [P, D])[:, :] for i in range(RING)]
        ge = [sg[1][:, i * F:(i + 1) * F] for i in range(2)]
        gg = [sg[1][:, (2 + i) * F:(3 + i) * F] for i in range(2)]
        gT = [sge[:, :], raw[0][:, :]]
        xh = [shi[i][:, 0:P] for i in range(2)]
        xl = [slo[i][:, 0:P] for i in range(2)]
        wk_s, wq_s, wv_s, wo_s = (n2[0][:, i * P:(i + 1) * P] for i in range(4))
        woT = n2[1][:, 0:P]
        bq_r = n2[1][:, P:2 * P]
        bv_r = n2[1][:, 2 * P:3 * P]
        bo_r = n2[1][:, 3 * P:4 * P]
        bcol = sb("bcol", [P, 2])
        ws_raw = sg[1][:, 0:2 * F]
        st1 = [sb(f"st1_{i}", [P, G, 6]) for i in range(2)]
        mv1 = [sb(f"mv1_{i}", [P, G, 2]) for i in range(2)]
        ve1 = [sb(f"ve1_{i}", [P, G]) for i in range(2)]
        rs1 = [sb(f"rs1_{i}", [P, G]) for i in range(2)]
        st2 = [sb(f"st2_{i}", [P, G, 6]) for i in range(2)]
        mv2 = [sb(f"mv2_{i}", [P, G, 2]) for i in range(2)]
        ve2 = [sb(f"ve2_{i}", [P, G]) for i in range(2)]
        rs2 = [sb(f"rs2_{i}", [P, G]) for i in range(2)]
        mx0 = sb("mx0", [P, G])
        nmx = sb("nmx", [P, G])
        sm = sb("sm", [P, G])
        rsm = sb("rsm", [P, G])
        lg = sb("lg", [P, E, B])
        cand = sb("cand", [P, E, B])
        cnt = sb("cnt", [P, E * B])
        oh = sb("oh", [P, E, B], BF16)
        iota_e = sb("iota_e", [P, E])
        best = sb("best", [P, B])
        tri = sb("tri", [P, P], BF16)
        ones_b = sb("ones_b", [P, P], BF16)
        ones_f = sb("ones_f", [P, 1])
        tot_i = sb("tot_i", [P, E], I32)
        ends = sb("ends", [P, E])
        tot = sb("tot", [P, E])
        tend = sb("tend", [P, E])
        shift = sb("shift", [P, E])
        pos_i = sb("pos_i", [P, B], I32)
        part_i = sb("part_i", [P, 2, B], I32)
        part = sb("part", [P, 2, B])
        iota_p = sb("iota_p", [P, P])
        iota_c = sb("iota_c", [P, TCOL])
        token = sb("token", [P, B])
        at_place, off_place = (xn, xnT), qT
        at_tile = [prT[:, 0:G * TCOL].rearrange("p (g c) -> p g c", g=G),
                   vb[:, 0:G * TCOL].rearrange("p (g c) -> p g c", g=G)]
        own = pr[:, 0:2 * TCOL].rearrange("p (a c) -> p a c", a=2)
        tcmp = sg[0][0:1, 0:TCOL * E].rearrange("p (c e) -> p c e", e=E)
        te_f = sg[0][0:1, TCOL * E:TCOL * (E + 1)]
        gid = sb("gid", [P, 2, TCOL], I32)
        te = sb("te", [1, TCOL], I32)
        gix = [sb(f"gix{i}", [P, 1], I32) for i in range(RING)]
        six = [sb(f"six{i}", [P, 1], I32) for i in range(RING)]

        names = """folds_loaded consts pool_consts dve_consts woT_ps woT_sb fold_ps fold_sb wshared_loaded
        w3_loaded wg_loaded half_split half_hi stats1 mv1_ready ve1_ready rstd1 xn_ready xnT_ps cxT_ps xnT_sb cxT_sb
        q_ps v_ps q_sb v_sb scores_ps max_ready nmax_ready exp_done rsum_ready probs_ready prT_ps prT_sb att_ps
        res_ready stats2 mv2_ready ve2_ready rstd2 n2_ready n2T_ps n2T_sb logits_ps logits_sb
        route onehot prefix_ps part_ready hilo_hi hilo_ready up_ps gelu_done inner_ready down_ps acc_ready
        place_off place_odd tile_marked table_ps table_ready
        gix_ready six_ready xT_ps x_hi x_ready r_up_ps r_gelu r_inner gT_ps gT_sb r_down_ps r_out
        act_passed dve_passed pool_passed""".split()
        S = {n: sem(n) for n in names}
        T = namedtuple("Sems", names)(**S)
        in_loaded = [sem(f"in_loaded{i}") for i in range(2)]
        raw_loaded = [sem(f"raw_loaded{i}") for i in range(2)]
        n2_stored = [sem(f"n2_stored{i}") for i in range(2)]
        acc_stored = [sem(f"acc_stored{i}") for i in range(2)]
        gathered = [sem(f"gathered{i}") for i in range(RING)]
        scattered = [sem(f"scattered{i}") for i in range(RING)]

        def b4(ap, w=D):
            return ap.rearrange("p (g d) -> p g d", g=G)

        def group(g):
            return bass.ds(g.n * G, G)

        def grp(h, off):
            return step(h, off, 2)

        def tile(h, off):
            return step(h, off, RING)

        def run_groups(eng, body, first=4, last=NG - 2):
            for i in range(0, first):
                body(grp(0, i), i)
            with eng.Fori(first // 2, last // 2) as h:
                for u in range(2):
                    body(grp(h, u), None)
            for i in range(last, NG):
                body(grp(0, i), i)

        def ahead(g, k):
            lap, slot = divmod(g.slot + k, 2)
            return Step(g.n + k, g.lap + lap, slot)

        def has(i, k):
            return i is None or 0 <= i + k < NG

        def t_ahead(t, k):
            lap, slot = divmod(t.slot + k, RING)
            return Step(t.n + k, t.lap + lap, slot)

        def t_has(s, k):
            return s is None or 0 <= s + k < TILES

        def run_routed(eng, slot, experts=None):
            first = 3
            loops = (TILES - RING + 1 - first) // RING
            def body(t, s, u):
                slot(t, s) if experts is None else slot(t, s, u)

            for s in range(-1, first):
                body(step(0, s, RING), s, s)
            with eng.Fori(0, loops) as h:
                if experts is not None:
                    experts.clear()
                for u in range(RING):
                    body(tile(h, first + u), None, u)
            if experts is not None:
                experts.clear()
            for s in range(first + loops * RING, TILES + 1):
                body(tile(0, s), s, s)

        def carry(eng, passed):
            eng.sem_inc(passed, 1)

        block = stack.enter_context(nc.Block())

        @block.sync
        def _(sp):
            for dst, src in ((wk_s, Wk), (wq_s, Wq), (wv_s, Wv), (wo_s, Wo)):
                sp.dma_start(dst, src).then_inc(T.folds_loaded, 16)
            sp.dma_start(bcol[:, 0:1], bq.rearrange("(p o) -> p o", o=1)).then_inc(T.folds_loaded, 16)
            sp.dma_start(bcol[:, 1:2], bv.rearrange("(p o) -> p o", o=1)).then_inc(T.folds_loaded, 16)
            sp.dma_start(bo_r, bo.rearrange("(o d) -> o d", o=1).to_broadcast([P, D])).then_inc(T.folds_loaded, 16)

            def load_inputs(g):
                if later_than(g, 2):
                    sp.wait_ge(T.stats1, g.n - 1)
                    sp.wait_ge(T.cxT_ps, g.n - 1)
                sp.dma_start(res[:, group(g), :], x_v[:, group(g), :]).then_inc(in_loaded[g.slot], 16)
                sp.dma_start(b4(cx[g.slot][:, :])[0:K], ctx_v[:, group(g), :]).then_inc(in_loaded[g.slot], 16)

            def load_half(n):
                if later_than(n, 2):
                    sp.wait_ge(T.half_split, n.n - 1)
                src = (W1, W2)[n.slot]
                sp.dma_start(raw[n.slot][:, :], src[bass.ds(n.lap, 1), :, :].rearrange("e p f -> p (e f)")
                             ).then_inc(raw_loaded[n.slot], 16)

            load_inputs(grp(0, 0))
            load_inputs(grp(0, 1))
            for dst, src in ((0, w1s), (1, w2s)):
                sp.dma_start(ws_raw[:, dst * F:(dst + 1) * F], src).then_inc(T.wshared_loaded, 16)
            sp.dma_start(wg[:, :], Wg).then_inc(T.wg_loaded, 16)
            sp.dma_start(w3[:, 0:E * NK * D].rearrange("p (s d) -> p s d", d=D),
                         W3.rearrange("e (k p) d -> p (e k) d", p=P)).then_inc(T.w3_loaded, 16)
            sp.dma_start(w3[:, E * NK * D:].rearrange("p (s d) -> p s d", d=D),
                         w3s.rearrange("(k p) d -> p k d", p=P)).then_inc(T.w3_loaded, 16)

            def body(g, i):
                if has(i, 2):
                    load_inputs(ahead(g, 2))
                if has(i, 0):
                    load_half(g)
                if has(i, -1):
                    c = ahead(g, -1)
                    sp.wait_ge(T.n2_ready, c.n + 1)
                    sp.dma_start(rows_v[:, group(c), D:2 * D], b4(n2[c.slot])).then_inc(n2_stored[c.slot], 16)

            def store_acc(g):
                sp.wait_ge(T.acc_ready, g.n + 1)
                sp.dma_start(rows_v[:, group(g), 0:D], res[:, group(g), :]).then_inc(acc_stored[g.slot], 16)

            def steps(g, i):
                body(g, i)
                if has(i, -3):
                    store_acc(ahead(g, -3))

            run_groups(sp, steps)
            for i in range(NG, NG + 3):
                steps(grp(0, i), i)
            for r in range(2):
                sp.wait_ge(acc_stored[r], 16 * (NG // 2))
                sp.wait_ge(n2_stored[r], 16 * (NG // 2))

        @block.gpsimd
        def _(pool):
            def const(ins):
                ins.then_inc(T.pool_consts, 1)
            const(nc.gpsimd.memset(ident[:, :], 0.0))
            const(nc.gpsimd.memset(ones_b[:, :], 1.0))
            const(nc.gpsimd.memset(neghalf[:, :], -0.5))
            const(nc.gpsimd.memset(ones_f[:, :], 1.0))
            const(nc.gpsimd.iota(iota_e[:, :], [[1, E]], base=0, channel_multiplier=0,
                                 allow_small_or_imprecise_dtypes=True))
            const(nc.gpsimd.iota(iota_p[:, :], [[1, P]], base=0, channel_multiplier=0,
                                 allow_small_or_imprecise_dtypes=True))
            const(nc.gpsimd.iota(iota_c[:, :], [[1, TCOL]], base=0, channel_multiplier=0,
                                 allow_small_or_imprecise_dtypes=True))
            const(nc.gpsimd.iota(token[:, :], [[P, B]], base=1, channel_multiplier=1,
                                 allow_small_or_imprecise_dtypes=True))
            pool.wait_ge(T.pool_consts, 8)
            nc.gpsimd.affine_select(out=ident[:, :], in_=ident[:, :], compare_op=ALU.not_equal, fill=1.0, base=0,
                                    pattern=[[-1, P]], channel_multiplier=1).then_inc(T.consts, 1)
            nc.gpsimd.affine_select(out=tri[:, :], in_=ones_b[:, :], compare_op=ALU.is_gt, fill=0.0, base=0,
                                    pattern=[[1, P]], channel_multiplier=-1).then_inc(T.consts, 1)

            def split(raw_ap, base, hi_sem, lo_sem, n):
                hi = w12[:, bass.ds(base, F)]
                nc.gpsimd.tensor_copy(hi, raw_ap).then_inc(hi_sem, 1)
                pool.wait_ge(hi_sem, n)
                nc.gpsimd.tensor_tensor(w12[:, bass.ds(base + F, F)], raw_ap, hi.bitcast(F32), ALU.subtract
                                        ).then_inc(lo_sem, 1)

            def rstd(mv, ve, rs, g, mv_ready, ve_ready, rs_ready):
                pool.wait_ge(mv_ready, g.n + 1)
                carry(pool, T.pool_passed)
                nc.gpsimd.tensor_scalar(ve[g.slot][:, :], mv[g.slot][:, :, 1], EPS, None, ALU.add
                                        ).then_inc(ve_ready, 1)
                pool.wait_ge(ve_ready, g.n + 1)
                nc.gpsimd.tensor_tensor(rs[g.slot][:, :], ve[g.slot][:, :], neghalf[:, :], ALU.pow
                                        ).then_inc(rs_ready, 1)

            def body(g, i):
                if has(i, 0):
                    pool.wait_ge(raw_loaded[g.slot], 16 * (g.lap + 1))
                    split(raw[g.slot][:, :], g.lap * 4 * F + g.slot * 2 * F, T.half_hi, T.half_split, g.n + 1)
                if has(i, 2):
                    rstd(mv1, ve1, rs1, ahead(g, 2), T.mv1_ready, T.ve1_ready, T.rstd1)
                if has(i, 0):
                    rstd(mv2, ve2, rs2, g, T.mv2_ready, T.ve2_ready, T.rstd2)

            for g in range(2):
                rstd(mv1, ve1, rs1, grp(0, g), T.mv1_ready, T.ve1_ready, T.rstd1)
            run_groups(pool, body)

            def slot(t, s):
                if t_has(s, -1):
                    o = t_ahead(t, -1)
                    pool.wait_ge(T.six_ready, o.n + 1)
                    pool.wait_ge(T.r_out, o.n + 1)
                    carry(pool, T.pool_passed)
                    nc.gpsimd.indirect_dma_start(
                        out_rows, bass.IndirectOffsetOnAxis(ap=six[o.slot][:, :], axis=0),
                        row_out[o.slot], None, bounds_check=TOK - 1, oob_is_err=False
                    ).then_inc(scattered[o.slot], 16)
                if t_has(s, RING - 1):
                    fetch(t_ahead(t, RING - 1))

            def fetch(t):
                pool.wait_ge(T.gix_ready, t.n + 1)
                carry(pool, T.pool_passed)
                nc.gpsimd.indirect_dma_start(
                    row_in[t.slot], None, rows, bass.IndirectOffsetOnAxis(ap=gix[t.slot][:, :], axis=0),
                    bounds_check=TOK - 1, oob_is_err=False).then_inc(gathered[t.slot], 16)

            pool.wait_ge(T.table_ready, 1)
            for r in range(2):
                pool.wait_ge(acc_stored[r], 16 * (NG // 2))
                pool.wait_ge(n2_stored[r], 16 * (NG // 2))
            for k in range(RING - 2):
                fetch(tile(0, k))
            run_routed(pool, slot)
            for r in range(RING):
                pool.wait_ge(scattered[r], 16 * ((TILES - r + RING - 1) // RING))

        @block.scalar
        def _(act):
            act.wait_ge(T.woT_ps, 1)
            nc.scalar.copy(woT, bank[0][:, 0:P]).then_inc(T.woT_sb, 1)

            def evac_in(g):
                act.wait_ge(T.xnT_ps, g.n + 1)
                if later_than(g, 1):
                    act.wait_ge(T.q_ps, g.n)
                nc.scalar.copy(xnT[:, :], bank[0][:, :]).then_inc(T.xnT_sb, 1)
                act.wait_ge(T.cxT_ps, g.n + 1)
                if later_than(g, 1):
                    act.wait_ge(T.scores_ps, g.n)
                nc.scalar.copy(cxT[:, :], bank[1][:, 0:G * K]).then_inc(T.cxT_sb, 1)

            def gelu(g, k):
                act.wait_ge(T.up_ps, NK * g.n + k + 1)
                if k or later_than(g, 1):
                    act.wait_ge(T.inner_ready, NK * g.n + k)
                nc.scalar.activation(sge[:, :], bank[2][:, :], ACT.Gelu).then_inc(T.gelu_done, 1)

            def queries(g):
                act.wait_ge(T.q_ps, g.n + 1)
                if later_than(g, 1):
                    act.wait_ge(T.scores_ps, g.n)
                nc.scalar.activation(qT[:, :], bank[0][:, :], ACT.Identity, bias=q_bias[:, :]).then_inc(T.q_sb, 1)

            def exponentials(g):
                act.wait_ge(T.nmax_ready, g.n + 1)
                if later_than(g, 1):
                    act.wait_ge(T.prT_ps, g.n)
                for j in range(G):
                    last = nc.scalar.activation(pr[:, j * K:(j + 1) * K], bank[4][:, j * K:(j + 1) * K],
                                                ACT.Exp, bias=nmx[:, j:j + 1], scale=SCALE,
                                                accum_out=sm[:, j:j + 1])
                last.then_inc(T.exp_done, 1)

            def body(g, i):
                c, s = ahead(g, -1), ahead(g, -2)
                if has(i, -2):
                    gelu(s, 0)
                if has(i, 0):
                    queries(g)
                if has(i, -2):
                    gelu(s, 1)
                if has(i, -1):
                    act.wait_ge(T.n2T_ps, c.n + 1)
                    if later_than(c, 1):
                        act.wait_ge(T.logits_ps, c.n)
                        act.wait_ge(T.hilo_ready, c.n)
                    nc.scalar.copy(n2T[:, :], bank[7][:, :]).then_inc(T.n2T_sb, 1)
                if has(i, -2):
                    gelu(s, 2)
                if has(i, 0):
                    exponentials(g)
                if has(i, 1):
                    evac_in(ahead(g, 1))
                if has(i, -2):
                    gelu(s, 3)
                if has(i, 0):
                    act.wait_ge(T.prT_ps, g.n + 1)
                    if later_than(g, 1):
                        act.wait_ge(T.att_ps, g.n)
                    nc.scalar.copy(prT[0:K, :], bank[4][0:K, :]).then_inc(T.prT_sb, 1)

            evac_in(grp(0, 0))
            run_groups(act, body)
            for i in range(NG, NG + 2):
                body(grp(0, i), i)

            def place(g):
                if later_than(g, 2):
                    act.wait_ge(T.place_odd, g.lap)
                    carry(act, T.act_passed)
                for j in range(G):
                    last = nc.scalar.activation(off_place[:, j * P:(j + 1) * P], iota_p[:, :], ACT.Abs,
                                                bias=part[:, 1, bass.ds(g.n * G + j, 1)], scale=-1.0)
                last.then_inc(T.place_off, 1)
                act.wait_ge(T.place_off, g.lap + 1)
                if later_than(g, 2):
                    act.wait_ge(T.table_ps, g.n - 1)
                nc.scalar.activation(at_place[1][:, :], off_place[:, :], ACT.Relu, bias=ones_f[:, :], scale=-1.0
                                     ).then_inc(T.place_odd, 1)

            act.wait_ge(T.part_ready, 1)
            place(grp(0, 1))
            with act.Fori(1, NG // 2) as h:
                place(grp(h, 1))

            def slot(t, s):
                if t_has(s, -1):
                    o = t_ahead(t, -1)
                    act.wait_ge(T.gT_ps, o.n + 1)
                    if later_than(o, 2):
                        act.wait_ge(T.r_down_ps, o.n - 1)
                    nc.scalar.copy(gT[o.slot % 2], bank[4 + o.slot % 2][:, :]).then_inc(T.gT_sb, 1)
                if t_has(s, 1):
                    o = t_ahead(t, 1)
                    act.wait_ge(T.r_up_ps, o.n + 1)
                    if later_than(o, 2):
                        act.wait_ge(T.r_inner, o.n - 1)
                    nc.scalar.activation(ge[o.slot % 2], bank[2 * (o.slot % 2)][:, :], ACT.Gelu
                                         ).then_inc(T.r_gelu, 1)

            run_routed(act, slot)

        @block.vector
        def _(dve):
            dve.wait_ge(T.folds_loaded, 7 * 16)
            nc.vector.tensor_copy(bq_r, bcol[:, 0:1].to_broadcast([P, P])).then_inc(T.dve_consts, 1)
            nc.vector.tensor_copy(bv_r, bcol[:, 1:2].to_broadcast([P, P])).then_inc(T.dve_consts, 1)
            dve.wait_ge(T.fold_ps, 1)
            nc.vector.tensor_copy(fold_q[:, :], bank[1][:, 0:P]).then_inc(T.fold_sb, 1)
            nc.vector.tensor_copy(q_bias[:, :], bank[1][:, P:P + 1]).then_inc(T.fold_sb, 1)
            dve.wait_ge(T.fold_ps, 2)
            nc.vector.tensor_copy(fold_v[:, :], bank[2][:, 0:P]).then_inc(T.fold_sb, 1)
            nc.vector.tensor_tensor(bb[:, :], bank[2][:, P:2 * P], bo_r, ALU.add).then_inc(T.fold_sb, 1)
            dve.wait_ge(T.wshared_loaded, 32)
            for w in range(2):
                base = E * 4 * F + w * 2 * F
                nc.vector.tensor_copy(w12[:, base:base + F], ws_raw[:, w * F:(w + 1) * F]).then_inc(T.hilo_hi, 1)
            dve.wait_ge(T.hilo_hi, 2)
            for w in range(2):
                base = E * 4 * F + w * 2 * F
                nc.vector.tensor_tensor(w12[:, base + F:base + 2 * F], ws_raw[:, w * F:(w + 1) * F],
                                        w12[:, base:base + F].bitcast(F32), ALU.subtract).then_inc(T.dve_consts, 1)

            def norm_stats(src, st, mv, g, stats, ready):
                for j in range(G):
                    last = nc.vector.bn_stats(st[g.slot][:, j, :], src(j))
                last.then_inc(stats, 1)
                dve.wait_ge(stats, g.n + 1)
                carry(dve, T.dve_passed)
                for j in range(G):
                    last = nc.vector.bn_aggr(mv[g.slot][:, j, :], st[g.slot][:, j, :])
                last.then_inc(ready, 1)

            def batch(g, j):
                return res[:, bass.ds(g.n * G + j, 1), :].rearrange("p o d -> p (o d)")

            def stats1(g):
                dve.wait_ge(in_loaded[g.slot], 32 * (g.lap + 1))
                if later_than(g, 2):
                    dve.wait_ge(T.rstd1, g.n - 1)
                carry(dve, T.dve_passed)
                norm_stats(lambda j: batch(g, j), st1, mv1, g, T.stats1, T.mv1_ready)

            def normalise(dst, mv, rs, g, ready):
                for j in range(G):
                    last = nc.vector.tensor_scalar(b4(dst)[:, j, :], batch(g, j), mv[g.slot][:, j, 0:1],
                                                   rs[g.slot][:, j:j + 1], ALU.subtract, ALU.mult)
                last.then_inc(ready, 1)

            def norm1(g):
                dve.wait_ge(T.rstd1, g.n + 1)
                if later_than(g, 1):
                    dve.wait_ge(T.xnT_ps, g.n)
                normalise(xn[:, :], mv1, rs1, g, T.xn_ready)

            def norm2(g):
                dve.wait_ge(T.rstd2, g.n + 1)
                if later_than(g, 2):
                    dve.wait_ge(T.n2T_ps, g.n - 1)
                    dve.wait_ge(n2_stored[g.slot], 16 * g.lap)
                normalise(n2[g.slot][:, :], mv2, rs2, g, T.n2_ready)

            def values(g):
                dve.wait_ge(T.v_ps, g.n + 1)
                if later_than(g, 1):
                    dve.wait_ge(T.att_ps, g.n)
                nc.vector.tensor_tensor(b4(vb[:, :])[0:K], b4(bank[1][:, :])[0:K],
                                        bb[0:K, :].unsqueeze(1).to_broadcast([K, G, D]), ALU.add
                                        ).then_inc(T.v_sb, 1)

            def maxima(g):
                dve.wait_ge(T.scores_ps, g.n + 1)
                nc.vector.reduce_max(mx0[:, :], bank[4][:, 0:G * K].rearrange("p (g k) -> p g k", g=G),
                                     AX.X).then_inc(T.max_ready, 1)
                if later_than(g, 1):
                    dve.wait_ge(T.exp_done, g.n)
                dve.wait_ge(T.max_ready, g.n + 1)
                nc.vector.tensor_scalar(nmx[:, :], mx0[:, :], -SCALE, None, ALU.mult
                                        ).then_inc(T.nmax_ready, 1)

            def probabilities(g):
                dve.wait_ge(T.exp_done, g.n + 1)
                nc.vector.reciprocal(rsm[:, :], sm[:, :]).then_inc(T.rsum_ready, 1)
                dve.wait_ge(T.rsum_ready, g.n + 1)
                pv = pr[:, :].rearrange("p (g k) -> p g k", g=G)
                nc.vector.tensor_tensor(pv, pv, rsm[:, :].unsqueeze(2).to_broadcast([P, G, K]), ALU.mult
                                        ).then_inc(T.probs_ready, 1)

            def residual(g):
                dve.wait_ge(T.att_ps, g.n + 1)
                nc.vector.tensor_tensor(res[:, group(g), :], res[:, group(g), :], b4(bank[7][:, :]), ALU.add
                                        ).then_inc(T.res_ready, 1)
                dve.wait_ge(T.res_ready, g.n + 1)
                if later_than(g, 2):
                    dve.wait_ge(T.rstd2, g.n - 1)
                carry(dve, T.dve_passed)
                norm_stats(lambda j: batch(g, j), st2, mv2, g, T.stats2, T.mv2_ready)

            def hilo(g):
                dve.wait_ge(T.n2T_sb, g.n + 1)
                if later_than(g, 2):
                    dve.wait_ge(T.up_ps, NK * (g.n - 1))
                nc.vector.tensor_copy(shi[g.slot][:, :], n2T[:, :]).then_inc(T.hilo_hi, 1)
                dve.wait_ge(T.hilo_hi, g.n + 3)
                nc.vector.tensor_tensor(slo[g.slot][:, :], n2T[:, :], shi[g.slot][:, :].bitcast(F32), ALU.subtract
                                        ).then_inc(T.hilo_ready, 1)

            def logits(g):
                dve.wait_ge(T.logits_ps, g.n + 1)
                nc.vector.tensor_copy(lg[:, :, group(g)], bank[5][:, 0:G * E].rearrange("p (g e) -> p e g", g=G)
                                      ).then_inc(T.logits_sb, 1)

            def inner(g, k):
                dve.wait_ge(T.gelu_done, NK * g.n + k + 1)
                if k == 0 and later_than(g, 2):
                    dve.wait_ge(T.down_ps, g.n - 1)
                nc.vector.tensor_tensor(sg[g.slot][:, k * 512:(k + 1) * 512], sge[:, :], bank[3][:, :], ALU.mult
                                        ).then_inc(T.inner_ready, 1)

            def accumulate(g):
                dve.wait_ge(T.down_ps, g.n + 1)
                nc.vector.tensor_tensor(res[:, group(g), :], res[:, group(g), :], b4(bank[6][:, :]), ALU.add
                                        ).then_inc(T.acc_ready, 1)

            def body(g, i):
                c, s, d = ahead(g, -1), ahead(g, -2), ahead(g, -3)
                if has(i, -2):
                    inner(s, 0)
                if has(i, 0):
                    values(g)
                if has(i, -1):
                    norm2(c)
                if has(i, -2):
                    inner(s, 1)
                if has(i, 0):
                    maxima(g)
                if has(i, 1):
                    norm1(ahead(g, 1))
                if has(i, -2):
                    inner(s, 2)
                if has(i, -1):
                    hilo(c)
                if has(i, 2):
                    stats1(ahead(g, 2))
                if has(i, 0):
                    probabilities(g)
                if has(i, -1):
                    logits(c)
                if has(i, -2):
                    inner(s, 3)
                if has(i, -3):
                    accumulate(d)
                if has(i, 0):
                    residual(g)

            stats1(grp(0, 0))
            dve.wait_ge(T.fold_sb, 4)
            norm1(grp(0, 0))
            stats1(grp(0, 1))
            run_groups(dve, body)
            body(grp(0, NG), NG)

            end = grp(0, NG - 1)
            def mark(g):
                if later_than(g, 2):
                    dve.wait_ge(T.table_ps, g.n - 1)
                if g.slot == 0:
                    nc.vector.tensor_tensor(b4(at_place[0][:, :]), iota_p[:, :].unsqueeze(1).to_broadcast([P, G, P]),
                                            part[:, 1, group(g)].unsqueeze(2).to_broadcast([P, G, P]), ALU.is_equal)
                for j in range(G):
                    i = bass.ds(g.n * G + j, 1)
                    last = nc.vector.tensor_scalar(at_tile[g.slot][:, j, :], iota_c[:, :], part[:, 0, i],
                                                   token[:, i], ALU.is_equal, ALU.mult)
                last.then_inc(T.tile_marked, 1)

            links = [0]

            def link(ins):
                links[0] += 1
                ins.then_inc(T.route, 1)
                dve.wait_ge(T.route, links[0])

            def by_tile(ap):
                return ap.rearrange("p e b -> p b e")

            dve.wait_ge(T.logits_sb, NG)
            link(nc.vector.reduce_max(best[:, :], by_tile(lg[:, :, :]), AX.X))
            link(nc.vector.tensor_tensor(lg[:, :, :], lg[:, :, :], best[:, :].unsqueeze(1).to_broadcast([P, E, B]),
                                         ALU.is_equal))
            link(nc.vector.tensor_scalar(lg[:, :, :], lg[:, :, :], -float(E), None, ALU.mult))
            link(nc.vector.tensor_tensor(cand[:, :, :], lg[:, :, :], iota_e[:, :].unsqueeze(2).to_broadcast([P, E, B]), ALU.add))
            link(nc.vector.tensor_reduce(best[:, :], by_tile(cand[:, :, :]), AX.X, ALU.min))
            nc.vector.tensor_tensor(oh[:, :, :], cand[:, :, :], best[:, :].unsqueeze(1).to_broadcast([P, E, B]),
                                    ALU.is_equal).then_inc(T.onehot, 1)
            inner(end, 0)
            accumulate(ahead(end, -1))
            dve.wait_ge(T.prefix_ps, 1)
            link(nc.vector.tensor_tensor_scan(cnt[:, :], ones_f[:, :].to_broadcast([P, E * B]), bank[0][:, :], 0.0, ALU.mult, ALU.add))
            inner(end, 1)
            cnt3 = cnt[:, :].rearrange("p (e b) -> p e b", e=E)
            link(nc.vector.tensor_copy(ends[:, :], cnt3[:, :, B - 1]))
            link(nc.vector.tensor_copy(tot[:, :], ends[:, :]))
            link(nc.vector.tensor_tensor(tot[:, 1:E], ends[:, 1:E], ends[:, 0:E - 1], ALU.subtract))
            link(nc.vector.tensor_scalar(tot_i[:, :], tot[:, :], float(P - 1), None, ALU.add))
            link(nc.vector.tensor_single_scalar(tot_i[:, :], tot_i[:, :], 7, ALU.arith_shift_right))
            link(nc.vector.tensor_copy(tot[:, :], tot_i[:, :]))
            link(nc.vector.tensor_tensor_scan(tend[:, :], ones_f[:, :].to_broadcast([P, E]), tot[:, :], 0.0, ALU.mult, ALU.add))
            link(nc.vector.memset(shift[:, 0:1], 0.0))
            link(nc.vector.tensor_scalar(shift[:, 1:E], tend[:, 0:E - 1], float(P), None, ALU.mult))
            link(nc.vector.tensor_tensor(shift[:, 1:E], shift[:, 1:E], ends[:, 0:E - 1], ALU.subtract))
            inner(end, 2)
            link(nc.vector.tensor_tensor(cnt[:, :], cnt[:, :], bank[0][:, :], ALU.subtract))
            link(nc.vector.tensor_tensor(cnt[:, :], cnt[:, :], bank[1][:, :], ALU.add))
            link(nc.vector.tensor_tensor(cnt3, cnt3, shift[:, :].unsqueeze(2).to_broadcast([P, E, B]), ALU.add))
            link(nc.vector.tensor_tensor(cnt3, cnt3, oh[:, :, :], ALU.mult))
            link(nc.vector.tensor_reduce(best[:, :], by_tile(cnt3), AX.X, ALU.add))
            link(nc.vector.tensor_copy(pos_i[:, :], best[:, :]))
            link(nc.vector.tensor_single_scalar(part_i[:, 0, :], pos_i[:, :], 7, ALU.arith_shift_right))
            link(nc.vector.tensor_single_scalar(part_i[:, 1, :], pos_i[:, :], P - 1, ALU.bitwise_and))
            link(nc.vector.tensor_copy(part[:, :, :], part_i[:, :, :]))
            dve.sem_inc(T.part_ready, 1)
            inner(end, 3)
            link(nc.vector.tensor_tensor(tcmp[:, :, :], iota_c[0:1, :].unsqueeze(2).to_broadcast([1, TCOL, E]),
                                         tend[0:1, :].unsqueeze(1).to_broadcast([1, TCOL, E]), ALU.is_ge))
            link(nc.vector.tensor_reduce(te_f[:, :], tcmp[:, :, :], AX.X, ALU.add))
            link(nc.vector.tensor_scalar(te[:, :], te_f[:, :], float(E - 1), None, ALU.min))

            mark(grp(0, 0))
            mark(grp(0, 1))
            accumulate(end)
            with dve.Fori(1, NG // 2) as h:
                mark(grp(h, 0))
                mark(grp(h, 1))
            dve.wait_ge(T.table_ps, NG)
            link(nc.vector.tensor_scalar(own[:, 0, :], bank[5][:, 0:TCOL], -1.0, None, ALU.add))
            link(nc.vector.tensor_scalar(own[:, 1, :], own[:, 0, :], 0.0, float(NOWHERE), ALU.is_lt, ALU.mult))
            link(nc.vector.tensor_scalar(own[:, 0, :], own[:, 0, :], 0.0, None, ALU.max))
            link(nc.vector.tensor_tensor(own[:, 1, :], own[:, 1, :], own[:, 0, :], ALU.add))
            nc.vector.tensor_copy(gid[:, :, :], own[:, :, :]).then_inc(T.table_ready, 1)

            def gather_ids(t):
                if later_than(t, RING):
                    dve.wait_ge(gathered[t.slot], 16 * t.lap)
                nc.vector.tensor_copy(gix[t.slot][:, :], gid[:, 0, bass.ds(t.n, 1)]).then_inc(T.gix_ready, 1)

            def scatter_ids(t):
                if later_than(t, RING):
                    dve.wait_ge(scattered[t.slot], 16 * t.lap)
                nc.vector.tensor_copy(six[t.slot][:, :], gid[:, 1, bass.ds(t.n, 1)]).then_inc(T.six_ready, 1)

            def slot(t, s):
                if t_has(s, 2):
                    parts(t_ahead(t, 2))
                if t_has(s, 1):
                    o = t_ahead(t, 1)
                    dve.wait_ge(T.r_gelu, o.n + 1)
                    if later_than(o, 2):
                        dve.wait_ge(T.gT_ps, o.n - 1)
                    nc.vector.tensor_tensor(gg[o.slot % 2], ge[o.slot % 2], bank[2 * (o.slot % 2) + 1][:, :],
                                            ALU.mult).then_inc(T.r_inner, 1)
                if t_has(s, -1):
                    o = t_ahead(t, -1)
                    dve.wait_ge(T.r_down_ps, o.n + 1)
                    if later_than(o, RING):
                        dve.wait_ge(scattered[o.slot], 16 * o.lap)
                    nc.vector.tensor_tensor(row_out[o.slot], row_in[o.slot][:, 0:D],
                                            bank[6][:, 0:P], ALU.add
                                            ).then_inc(T.r_out, 1)
                if t_has(s, 0):
                    scatter_ids(t)
                if t_has(s, RING):
                    gather_ids(t_ahead(t, RING))

            def parts(t):
                dve.wait_ge(T.xT_ps, t.n + 1)
                if later_than(t, 2):
                    dve.wait_ge(T.r_up_ps, t.n - 1)
                src = bank[7][:, 0:P]
                nc.vector.tensor_copy(xh[t.slot % 2], src).then_inc(T.x_hi, 1)
                dve.wait_ge(T.x_hi, t.n + 1)
                nc.vector.tensor_tensor(xl[t.slot % 2], src, xh[t.slot % 2].bitcast(F32), ALU.subtract
                                        ).then_inc(T.x_ready, 1)

            dve.wait_ge(T.table_ready, 1)
            for k in range(RING - 1):
                gather_ids(tile(0, k))
            parts(tile(0, 0))
            run_routed(dve, slot)

        @block.tensor
        def _(pe):
            mm, tr = nc.tensor.matmul, nc.tensor.transpose
            pe.wait_ge(T.consts, 2)
            pe.wait_ge(T.folds_loaded, 7 * 16)
            tr(bank[0][:, 0:P], wo_s, ident[:, :]).then_inc(T.woT_ps, 1)
            pe.wait_ge(T.dve_consts, 2)
            mm(bank[1][:, 0:P], wq_s, wk_s, start=True, stop=True)
            mm(bank[1][:, P:2 * P], wk_s, bq_r, start=True, stop=True).then_inc(T.fold_ps, 1)
            pe.wait_ge(T.woT_sb, 1)
            mm(bank[2][:, 0:P], wv_s, woT, start=True, stop=True)
            mm(bank[2][:, P:2 * P], bv_r, woT, start=True, stop=True).then_inc(T.fold_ps, 1)
            pe.wait_ge(T.fold_sb, 4)

            def transpose_in(g):
                pe.wait_ge(T.xn_ready, g.n + 1)
                if later_than(g, 1):
                    pe.wait_ge(T.q_sb, g.n)
                for j in range(G):
                    last = tr(bank[0][:, j * P:(j + 1) * P], b4(xn[:, :])[:, j, :], ident[:, :])
                last.then_inc(T.xnT_ps, 1)
                pe.wait_ge(in_loaded[g.slot], 32 * (g.lap + 1))
                if later_than(g, 1):
                    pe.wait_ge(T.v_sb, g.n)
                for j in range(G):
                    last = tr(bank[1][:, j * K:(j + 1) * K], b4(cx[g.slot][:, :])[0:K, j, :], ident[0:K, 0:K])
                last.then_inc(T.cxT_ps, 1)

            def project(g):
                pe.wait_ge(T.xnT_sb, g.n + 1)
                mm(bank[0][:, :], fold_q[:, :], xnT[:, :], start=True, stop=True).then_inc(T.q_ps, 1)
                pe.wait_ge(T.cxT_sb, g.n + 1)
                for j in range(G):
                    last = mm(bank[1][0:K, j * D:(j + 1) * D], cxT[:, j * K:(j + 1) * K], fold_v[:, :],
                              start=True, stop=True)
                last.then_inc(T.v_ps, 1)

            def scores(g):
                pe.wait_ge(T.q_sb, g.n + 1)
                if later_than(g, 1):
                    pe.wait_ge(T.prT_sb, g.n)
                for j in range(G):
                    last = mm(bank[4][:, j * K:(j + 1) * K], qT[:, j * P:(j + 1) * P],
                              cxT[:, j * K:(j + 1) * K], start=True, stop=True)
                last.then_inc(T.scores_ps, 1)

            def transpose_probs(g):
                pe.wait_ge(T.probs_ready, g.n + 1)
                for j in range(G):
                    last = tr(bank[4][0:K, j * P:(j + 1) * P], pr[:, j * K:(j + 1) * K], ident[:, :])
                last.then_inc(T.prT_ps, 1)

            def attend(g):
                pe.wait_ge(T.prT_sb, g.n + 1)
                pe.wait_ge(T.v_sb, g.n + 1)
                if later_than(g, 1):
                    pe.wait_ge(T.n2T_sb, g.n)
                for j in range(G):
                    last = mm(bank[7][:, j * D:(j + 1) * D], prT[0:K, j * P:(j + 1) * P],
                              vb[0:K, j * D:(j + 1) * D], start=True, stop=True)
                last.then_inc(T.att_ps, 1)

            def transpose_n2(g):
                pe.wait_ge(T.n2_ready, g.n + 1)
                for j in range(G):
                    last = tr(bank[7][:, j * P:(j + 1) * P], n2[g.slot][:, j * D:(j + 1) * D], ident[:, :])
                last.then_inc(T.n2T_ps, 1)

            def logits(g):
                pe.wait_ge(T.n2T_sb, g.n + 1)
                if later_than(g, 1):
                    pe.wait_ge(T.logits_sb, g.n)
                for j in range(G):
                    last = mm(bank[5][:, j * E:(j + 1) * E], n2T[:, j * P:(j + 1) * P], wg[:, :],
                              start=True, stop=True)
                last.then_inc(T.logits_ps, 1)

            def up(g, k):
                if k == 0:
                    pe.wait_ge(T.hilo_ready, g.n + 1)
                if k or later_than(g, 1):
                    pe.wait_ge(T.inner_ready, NK * g.n + k)
                for w in range(2):
                    base = E * 4 * F + w * 2 * F + k * P
                    hi, lo = w12[:, base:base + P], w12[:, base + F:base + F + P]
                    dst = bank[2 + w][:, :]
                    mm(dst, hi, shi[g.slot][:, :], start=True, stop=False)
                    mm(dst, hi, slo[g.slot][:, :], start=False, stop=False)
                    last = mm(dst, lo, shi[g.slot][:, :], start=False, stop=True)
                last.then_inc(T.up_ps, 1)

            def down(g, half):
                if half == 0:
                    pe.wait_ge(T.inner_ready, NK * (g.n + 1))
                    if later_than(g, 1):
                        pe.wait_ge(T.acc_ready, g.n)
                for j in range(2 * half, 2 * half + 2):
                    for k in range(NK):
                        last = mm(bank[6][:, j * D:(j + 1) * D], sg[g.slot][:, k * 512 + j * P:k * 512 + (j + 1) * P],
                                  w3[:, (E * NK + k) * D:(E * NK + k + 1) * D], start=k == 0, stop=k == NK - 1)
                if half:
                    last.then_inc(T.down_ps, 1)

            def body(g, i):
                c, s, d = ahead(g, -1), ahead(g, -2), ahead(g, -3)
                if has(i, -2):
                    up(s, 0)
                if has(i, 0):
                    project(g)
                if has(i, -2):
                    up(s, 1)
                if has(i, 0):
                    scores(g)
                if has(i, -1):
                    transpose_n2(c)
                if has(i, -2):
                    up(s, 2)
                if has(i, -3):
                    down(d, 0)
                if has(i, 1):
                    transpose_in(ahead(g, 1))
                if has(i, -2):
                    up(s, 3)
                if has(i, -1):
                    logits(c)
                if has(i, 0):
                    transpose_probs(g)
                if has(i, -3):
                    down(d, 1)
                if has(i, 0):
                    attend(g)

            transpose_in(grp(0, 0))
            pe.wait_ge(T.wg_loaded, 16)
            pe.wait_ge(T.w3_loaded, 32)
            pe.wait_ge(T.dve_consts, 4)
            run_groups(pe, body)
            body(grp(0, NG), NG)

            end = grp(0, NG - 1)
            up(end, 0)
            down(ahead(end, -1), 0)
            down(ahead(end, -1), 1)
            pe.wait_ge(T.onehot, 1)
            oh_f = oh[:, :, :].rearrange("p e b -> p (e b)")
            mm(bank[0][:, :], ones_b[:, :], oh_f, start=True, stop=True)
            mm(bank[1][:, :], tri[:, :], oh_f, start=True, stop=True).then_inc(T.prefix_ps, 1)
            for k in range(1, NK):
                up(end, k)
            down(end, 0)
            down(end, 1)

            def table(g, first=False, final=False):
                if g.slot:
                    pe.wait_ge(T.place_odd, g.lap + 1)
                pe.wait_ge(T.tile_marked, g.n + 1)
                for j in range(G):
                    last = mm(bank[5][:, 0:TCOL], at_place[g.slot][:, j * P:(j + 1) * P], at_tile[g.slot][:, j, :],
                              start=first and j == 0, stop=final and j == G - 1)
                last.then_inc(T.table_ps, 1)

            table(grp(0, 0), first=True)
            table(grp(0, 1))
            with pe.Fori(1, NG // 2 - 1) as h:
                table(grp(h, 0))
                table(grp(h, 1))
            table(grp(0, NG - 2))
            table(end, final=True)

            def fetch_T(t):
                pe.wait_ge(gathered[t.slot], 16 * (t.lap + 1))
                if later_than(t, 1):
                    pe.wait_ge(T.x_ready, t.n)
                tr(bank[7][:, 0:P], row_in[t.slot][:, D:2 * D], ident[:, :]
                   ).then_inc(T.xT_ps, 1)

            experts = {}

            def expert(t, s, u):
                if u not in experts:
                    experts[u] = pe.value_load(te[0:1, bass.ds(t.n, 1)], min_val=0, max_val=E - 1)
                return experts[u]

            def r_up(t, e):
                pe.wait_ge(T.x_ready, t.n + 1)
                if later_than(t, 2):
                    pe.wait_ge(T.r_inner, t.n - 1)
                q = t.slot % 2
                for w in range(2):
                    hi = w12[:, bass.ds(e * (4 * F) + w * 2 * F, F)]
                    lo = w12[:, bass.ds(e * (4 * F) + w * 2 * F + F, F)]
                    dst = bank[2 * q + w][:, :]
                    mm(dst, xh[q], hi, start=True, stop=False)
                    mm(dst, xh[q], lo, start=False, stop=False)
                    last = mm(dst, xl[q], hi, start=False, stop=True)
                last.then_inc(T.r_up_ps, 1)

            def slot(t, s, u):
                if t_has(s, -1):
                    o = t_ahead(t, -1)
                    pe.wait_ge(T.r_inner, o.n + 1)
                    if later_than(o, 2):
                        pe.wait_ge(T.gT_sb, o.n - 1)
                    for k in range(NK):
                        last = tr(bank[4 + o.slot % 2][:, k * P:(k + 1) * P], gg[o.slot % 2][:, k * P:(k + 1) * P],
                                  ident[:, :])
                    last.then_inc(T.gT_ps, 1)
                if t_has(s, 2):
                    fetch_T(t_ahead(t, 2))
                if t_has(s, 1):
                    r_up(t_ahead(t, 1), expert(t_ahead(t, 1), s, u + 1))
                if t_has(s, -1):
                    e = expert(o, s, u - 1)
                    pe.wait_ge(T.gT_sb, o.n + 1)
                    if later_than(o, 1):
                        pe.wait_ge(T.r_out, o.n)
                    for k in range(NK):
                        last = mm(bank[6][:, 0:P],
                                  gT[o.slot % 2][:, k * P:(k + 1) * P],
                                  w3[:, bass.ds(e * (NK * D) + k * D, D)], start=k == 0, stop=k == NK - 1)
                    last.then_inc(T.r_down_ps, 1)

            pe.wait_ge(T.table_ready, 1)
            pe.wait_ge(T.half_split, NG)
            fetch_T(tile(0, 0))
            run_routed(pe, slot, experts)


_INS = ['x', 'ctx_1024', 'L0_xattn_Wk', 'L0_xattn_Wv', 'L0_xattn_bv', 'L0_xattn_Wq', 'L0_xattn_bq', 'L0_xattn_Wo',
        'L0_xattn_bo', 'L0_ffn_w1s', 'L0_ffn_w2s', 'L0_ffn_w3s', 'L0_ffn_W1', 'L0_ffn_W2', 'L0_ffn_W3', 'L0_ffn_Wg']


def kernel(**inputs):
    import concourse.bacc as bacc
    from concourse.bass_utils import run_bass_kernel_spmd

    nc = bacc.Bacc("TRN2", target_bir_lowering=False, num_devices=1)
    arrays, args = {}, []
    for name in _INS:
        a = np.ascontiguousarray(inputs[name])
        arrays[name] = a
        args.append(nc.dram_tensor(name, a.shape, mybir.dt.from_np(a.dtype), kind="ExternalInput").ap())
    args.append(nc.dram_tensor("y", (B, P, D), F32, kind="ExternalOutput").ap())
    xattn_moe(nc, *args)
    r = run_bass_kernel_spmd(nc, [arrays], core_ids=[0])
    return r.results[0]["y"]
```

```python
from collections import namedtuple
from contextlib import ExitStack

import numpy as np
import concourse.bass as bass
from concourse import mybir

F32 = mybir.dt.float32
F32R = mybir.dt.float32r
BF16 = mybir.dt.bfloat16
I32 = mybir.dt.int32
ALU = mybir.AluOpType
ACT = mybir.ActivationFunctionType
AX = mybir.AxisListType

P = 128
B, K, D = 64, 77, 128
G = 4
NG = B // G
E, F = 8, 512
NK = F // P
TOK = B * P
R = 2 * P
TILES = (TOK + E * (R - 1)) // R
ROW = 2 * D + 1
PAD_TILES = TOK // R + 1
LIST_TILES = E * PAD_TILES + 1
RING = 6
EPS = 1e-5
SCALE = 1.0 / float(np.sqrt(np.float32(D)))
LAST_BANKS = (6, 4, 2, 7)
T_BANKS = (7, 4)
NOWHERE = 4 * TOK

Step = namedtuple("Step", "n lap slot")


def step(h, off, ring):
    lap, slot = divmod(off, ring)
    return Step(h * ring + off, h + lap, slot)


def later_than(s, k):
    return not isinstance(s.n, int) or s.n >= k


def xattn_moe(nc, x, ctx_in, Wk, Wv, bv, Wq, bq, Wo, bo, w1s, w2s, w3s, W1, W2, W3, Wg, out):
    x_v = x.rearrange("b p d -> p b d")
    ctx_v = ctx_in.rearrange("b k d -> k b d")
    out_rows = out.rearrange("b p d -> (b p) d")
    rows = nc.dram_tensor("token_rows", (LIST_TILES * R, ROW), F32).ap()

    with ExitStack() as stack:
        def sb(name, shape, dt=F32):
            return stack.enter_context(nc.sbuf_tensor(name, shape, dt))

        def sem(name):
            return stack.enter_context(nc.semaphore(name))

        bank = [stack.enter_context(nc.psum_tensor(f"bank{i}", [P, 512], F32)) for i in range(8)]

        w12 = sb("w12", [P, (E + 1) * 4 * F], F32R)
        w3 = sb("w3", [P, (E + 1) * NK * D])
        wg = sb("wg", [P, E])
        ident = sb("ident", [P, P])
        neghalf = sb("neghalf", [P, G])
        bb = sb("bb", [P, D])
        fold_q = sb("fold_q", [P, P])
        fold_v = sb("fold_v", [P, P])
        q_bias = sb("q_bias", [P, 1])
        res = sb("res", [P, B, D])
        raw = [sb(f"raw{i}", [P, F]) for i in range(2)]
        cx = [sb(f"cx{i}", [P, G * D]) for i in range(2)]
        xn = sb("xn", [P, G * D])
        xnT = sb("xnT", [P, G * P])
        cxT = sb("cxT", [P, G * K])
        qT = sb("qT", [P, G * P])
        pr = sb("pr", [P, G * K])
        prT = sb("prT", [P, G * P])
        vb = sb("vb", [P, G * D])
        n2 = [sb(f"n2_{i}", [P, G * D]) for i in range(2)]
        n2T = sb("n2T", [P, G * P])
        parts_s = sb("parts_s", [P, 4 * G * P], F32R)
        shi = [parts_s[:, i * G * P:(i + 1) * G * P] for i in (0, 1)]
        slo = [parts_s[:, i * G * P:(i + 1) * G * P] for i in (2, 3)]
        sg = [sb(f"sg{i}", [P, NK * G * P]) for i in range(2)]
        sge = sb("sge", [P, G * P])
        stage = [sb(f"stage{i}", [P, G * ROW]) for i in range(2)]
        padding = sb("padding", [P, ROW])
        spent = res[:, :, :].rearrange("p b d -> p (b d)")
        w12_t = [w12[:, E * 4 * F:(E + 1) * 4 * F], parts_s[:, :]]
        w3_t = [spent[:, i * F:(i + 1) * F] for i in range(2)]
        row_in = [spent[:, 2 * F + i * 2 * ROW:2 * F + (i + 1) * 2 * ROW].rearrange("p (j c) -> p j c", j=2)
                  for i in range(RING)]
        row_out = [t[:, i * R:(i + 1) * R] for t in (xn, xnT, qT) for i in range(RING // 3)]
        ge = [sge[:, :], raw[0][:, :]]
        gg = [sg[1][:, i * NK * R:(i + 1) * NK * R] for i in range(2)]
        xh = [sb(f"xh{i}", [P, R], F32R) for i in range(2)]
        xl = [sb(f"xl{i}", [P, R], F32R) for i in range(2)]
        wk_s, wq_s, wv_s, wo_s = (n2[0][:, i * P:(i + 1) * P] for i in range(4))
        woT = n2[1][:, 0:P]
        bq_r = n2[1][:, P:2 * P]
        bv_r = n2[1][:, 2 * P:3 * P]
        bo_r = n2[1][:, 3 * P:4 * P]
        bcol = sb("bcol", [P, 2])
        ws_raw = sg[1][:, 0:2 * F]
        st1 = [sb(f"st1_{i}", [P, G, 6]) for i in range(2)]
        mv1 = [sb(f"mv1_{i}", [P, G, 2]) for i in range(2)]
        ve1 = [sb(f"ve1_{i}", [P, G]) for i in range(2)]
        rs1 = [sb(f"rs1_{i}", [P, G]) for i in range(2)]
        st2 = [sb(f"st2_{i}", [P, G, 6]) for i in range(2)]
        mv2 = [sb(f"mv2_{i}", [P, G, 2]) for i in range(2)]
        ve2 = [sb(f"ve2_{i}", [P, G]) for i in range(2)]
        nm2 = [sb(f"nm2_{i}", [P, G]) for i in range(2)]
        rs2 = sb("rs2", [P, B])
        nb2 = sb("nb2", [P, B])
        mx0 = sb("mx0", [P, G])
        nmx = sb("nmx", [P, G])
        sm = sb("sm", [P, G])
        rsm = sb("rsm", [P, G])
        best = sb("best", [P, G])
        is_best = sb("is_best", [P, G, E])
        weight = sb("weight", [P, E])
        win = sb("win", [P, G])
        oh = [sb(f"oh{i}", [P, G, E], BF16) for i in range(2)]
        tri = sb("tri", [P, P], BF16)
        rest = sb("rest", [P, P], BF16)
        ones_b = sb("ones_b", [P, P], BF16)
        ones_f = sb("ones_f", [P, 1])
        negone = sb("negone", [P, G])
        start_e = sb("start_e", [P, E])
        start_b = sb("start_b", [P, G, E], BF16)
        at_row = sb("at_row", [P, G, E])
        pos_f = sb("pos_f", [P, G])
        pos = [sb(f"pos{i}", [P, G], I32) for i in range(2)]
        numbers = sb("numbers", [P, B], I32)
        pad_i = sb("pad_i", [1, E], I32)
        cnt_i = sb("cnt_i", [1, E], I32)
        cnt = sb("cnt", [1, E])
        tend = sb("tend", [1, E])
        spare = sb("spare", [1, E])
        iota_t = sb("iota_t", [1, TILES])
        tcmp = sg[0][0:1, 0:TILES * E].rearrange("p (c e) -> p c e", e=E)
        tskip = sg[0][0:1, TILES * E:2 * TILES * E].rearrange("p (c e) -> p c e", e=E)
        te_f = sb("te_f", [1, TILES])
        to_f = sb("to_f", [1, TILES])
        te = sb("te", [1, TILES], I32)
        to = sb("to", [1, TILES], I32)

        names = """folds_loaded bo_loaded consts pool_consts dve_consts woT_ps woT_sb fold_ps fold_sb wshared_loaded
        w3_loaded w3s_loaded wg_loaded half_split half_hi stats1 mv1_ready ve1_ready rstd1 xn_ready xnT_ps cxT_ps xnT_sb cxT_sb
        q_ps v_ps q_sb v_sb scores_ps max_ready nmax_ready exp_done rsum_ready probs_ready prT_ps prT_sb att_ps
        res_ready stats2 mv2_ready ve2_ready nm2_ready rstd2 nb2_ready n2_ready n2T_ps n2T_sb logits_ps logits_read
        choice onehot ranks_ps ranks_read pos_summed pos_ready counted
        hilo_hi hilo_ready up_ps gelu_done inner_ready down_ps acc_ready batch_down_ps batch_acc
        n2_staged id_staged stage_free lists_full pads_ready tiles_ready padded
        xT_ps x_hi x_ready w12_copied w3_copied r_up_ps r_gelu r_inner r_down_ps r_out
        act_passed dve_passed pool_passed""".split()
        S = {n: sem(n) for n in names}
        T = namedtuple("Sems", names)(**S)
        in_loaded = [sem(f"in_loaded{i}") for i in range(2)]
        raw_loaded = [sem(f"raw_loaded{i}") for i in range(2)]
        listed = [sem(f"listed{i}") for i in range(2)]
        tile_loaded = [sem(f"tile_loaded{i}") for i in range(RING)]
        scattered = [sem(f"scattered{i}") for i in range(RING)]

        def b4(ap, w=D):
            return ap.rearrange("p (g d) -> p g d", g=G)

        def group(g):
            return bass.ds(g.n * G, G)

        def batch(g, j):
            return res[:, bass.ds(g.n * G + j, 1), :].rearrange("p o d -> p (o d)")

        def grp(h, off):
            return step(h, off, 2)

        def tile(h, off):
            return step(h, off, RING)

        def run_groups(eng, body, first=4, last=NG - 2):
            for i in range(0, first):
                body(grp(0, i), i)
            with eng.Fori(first // 2, last // 2) as h:
                for u in range(2):
                    body(grp(h, u), None)
            for i in range(last, NG):
                body(grp(0, i), i)

        def ahead(g, k):
            lap, slot = divmod(g.slot + k, 2)
            return Step(g.n + k, g.lap + lap, slot)

        def has(i, k):
            return i is None or 0 <= i + k < NG

        def t_ahead(t, k):
            lap, slot = divmod(t.slot + k, RING)
            return Step(t.n + k, t.lap + lap, slot)

        def t_has(s, k):
            return s is None or 0 <= s + k < TILES

        first = RING + 2
        loops = (TILES - 2 - first) // RING

        def run_routed(eng, slot):
            for s in range(-1, first):
                slot(step(0, s, RING), s)
            with eng.Fori(0, loops) as h:
                for u in range(RING):
                    slot(tile(h, first + u), None)
            for s in range(first + loops * RING, TILES):
                slot(tile(0, s), s)

        def carry(eng, passed):
            eng.sem_inc(passed, 1)

        block = stack.enter_context(nc.Block())

        @block.sync
        def _(sp):
            def load_inputs(g):
                if later_than(g, 2):
                    sp.wait_ge(T.stats1, g.n - 1)
                    sp.wait_ge(T.cxT_ps, g.n - 1)
                sp.dma_start(res[:, group(g), :], x_v[:, group(g), :]).then_inc(in_loaded[g.slot], 16)
                sp.dma_start(b4(cx[g.slot][:, :])[0:K], ctx_v[:, group(g), :]).then_inc(in_loaded[g.slot], 16)

            def load_half(n):
                if later_than(n, 2):
                    sp.wait_ge(T.half_split, n.n - 1)
                src = (W1, W2)[n.slot]
                sp.dma_start(raw[n.slot][:, :], src[bass.ds(n.lap, 1), :, :].rearrange("e p f -> p (e f)")
                             ).then_inc(raw_loaded[n.slot], 16)

            load_inputs(grp(0, 0))
            for dst, src in ((wq_s, Wq), (wk_s, Wk)):
                sp.dma_start(dst, src).then_inc(T.folds_loaded, 16)
            load_inputs(grp(0, 1))
            for dst, src in ((0, w1s), (1, w2s)):
                sp.dma_start(ws_raw[:, dst * F:(dst + 1) * F], src).then_inc(T.wshared_loaded, 16)
            sp.dma_start(wg[:, :], Wg).then_inc(T.wg_loaded, 16)
            sp.dma_start(w3[:, E * NK * D:].rearrange("p (s d) -> p s d", d=D),
                         w3s.rearrange("(k p) d -> p k d", p=P)).then_inc(T.w3s_loaded, 16)

            def body(g, i):
                if has(i, 2):
                    load_inputs(ahead(g, 2))
                if has(i, 0):
                    load_half(g)

            run_groups(sp, body)
            sp.dma_start(w3[:, 0:E * NK * D].rearrange("p (s d) -> p s d", d=D),
                         W3.rearrange("e (k p) d -> p (e k) d", p=P)).then_inc(T.w3_loaded, 16)

            sp.wait_ge(T.pool_consts, 16)
            def pad(row):
                sp.dma_start(rows[bass.ds(row, R), :].rearrange("(j p) c -> p j c", j=2),
                             padding[:, :].unsqueeze(1).to_broadcast([P, 2, ROW])).then_inc(T.padded, 16)

            pad(E * PAD_TILES * R)
            sp.wait_ge(T.pads_ready, 1)
            for e in range(E):
                pad(sp.value_load(pad_i[0:1, e:e + 1], min_val=0, max_val=(LIST_TILES - 1) * R))

            def load_tile(t, first=False):
                row = sp.value_load(to[0:1, bass.ds(t.n, 1)], min_val=0, max_val=(LIST_TILES - 1) * R)
                if first:
                    sp.wait_ge(T.padded, (E + 1) * 16)
                    sp.wait_ge(T.lists_full, 1)
                if later_than(t, RING):
                    sp.wait_ge(scattered[t.slot], 32 * t.lap)
                sp.dma_start(row_in[t.slot], rows[bass.ds(row, R), :].rearrange("(j p) c -> p j c", j=2)
                             ).then_inc(tile_loaded[t.slot], 16)

            sp.wait_ge(T.tiles_ready, 1)
            for k in range(RING):
                load_tile(tile(0, k), first=k == 0)
            with sp.Fori(1, TILES // RING) as h:
                for u in range(RING):
                    load_tile(tile(h, u))
            for k in range(TILES // RING * RING, TILES):
                load_tile(tile(0, k))

        @block.gpsimd
        def _(pool):
            def const(ins):
                ins.then_inc(T.pool_consts, 1)
            const(nc.gpsimd.memset(ident[:, :], 0.0))
            const(nc.gpsimd.memset(ones_b[:, :], 1.0))
            const(nc.gpsimd.memset(neghalf[:, :], -0.5))
            const(nc.gpsimd.memset(ones_f[:, :], 1.0))
            const(nc.gpsimd.memset(negone[:, :], -1.0))
            const(nc.gpsimd.memset(padding[:, 0:2 * D], 0.0))
            const(nc.gpsimd.memset(padding[:, 2 * D:ROW].bitcast(I32), NOWHERE))
            for g in range(G):
                const(nc.gpsimd.iota(start_b[:, g, :], [[PAD_TILES * R // P, E]], base=0, channel_multiplier=0,
                                     allow_small_or_imprecise_dtypes=True))
            const(nc.gpsimd.iota(weight[:, :], [[-1, E]], base=E, channel_multiplier=0,
                                 allow_small_or_imprecise_dtypes=True))
            const(nc.gpsimd.iota(start_e[:, :], [[PAD_TILES * R, E]], base=0, channel_multiplier=0,
                                 allow_small_or_imprecise_dtypes=True))
            const(nc.gpsimd.iota(iota_t[:, :], [[1, TILES]], base=0, channel_multiplier=0,
                                 allow_small_or_imprecise_dtypes=True))
            const(nc.gpsimd.iota(numbers[:, :], [[P, B]], base=0, channel_multiplier=1))
            pool.sem_inc(T.pool_consts, 1)
            pool.wait_ge(T.pool_consts, 16)
            nc.gpsimd.affine_select(out=ident[:, :], in_=ident[:, :], compare_op=ALU.not_equal, fill=1.0, base=0,
                                    pattern=[[-1, P]], channel_multiplier=1).then_inc(T.consts, 1)
            nc.gpsimd.affine_select(out=tri[:, :], in_=ones_b[:, :], compare_op=ALU.is_gt, fill=0.0, base=0,
                                    pattern=[[1, P]], channel_multiplier=-1).then_inc(T.consts, 1)
            nc.gpsimd.affine_select(out=rest[:, :], in_=ones_b[:, :], compare_op=ALU.is_ge, fill=0.0, base=0,
                                    pattern=[[-1, P]], channel_multiplier=1).then_inc(T.consts, 1)
            pool.sem_inc(T.stage_free, 2)

            def split(raw_ap, base, hi_sem, lo_sem, n):
                hi = w12[:, bass.ds(base, F)]
                nc.gpsimd.tensor_copy(hi, raw_ap).then_inc(hi_sem, 1)
                pool.wait_ge(hi_sem, n)
                nc.gpsimd.tensor_tensor(w12[:, bass.ds(base + F, F)], raw_ap, hi.bitcast(F32), ALU.subtract
                                        ).then_inc(lo_sem, 1)

            def rstd1(g):
                pool.wait_ge(T.mv1_ready, g.n + 1)
                carry(pool, T.pool_passed)
                nc.gpsimd.tensor_scalar(ve1[g.slot][:, :], mv1[g.slot][:, :, 1], EPS, None, ALU.add
                                        ).then_inc(T.ve1_ready, 1)
                pool.wait_ge(T.ve1_ready, g.n + 1)
                nc.gpsimd.tensor_tensor(rs1[g.slot][:, :], ve1[g.slot][:, :], neghalf[:, :], ALU.pow
                                        ).then_inc(T.rstd1, 1)

            def rstd2(g):
                pool.wait_ge(T.mv2_ready, g.n + 1)
                carry(pool, T.pool_passed)
                nc.gpsimd.tensor_scalar(ve2[g.slot][:, :], mv2[g.slot][:, :, 1], EPS, None, ALU.add
                                        ).then_inc(T.ve2_ready, 1)
                pool.wait_ge(T.ve2_ready, g.n + 1)
                carry(pool, T.pool_passed)
                nc.gpsimd.tensor_tensor(rs2[:, group(g)], ve2[g.slot][:, :], neghalf[:, :], ALU.pow
                                        ).then_inc(T.rstd2, 1)
                nc.gpsimd.tensor_tensor(nm2[g.slot][:, :], mv2[g.slot][:, :, 0], negone[:, :], ALU.mult
                                        ).then_inc(T.nm2_ready, 1)
                pool.wait_ge(T.nm2_ready, g.n + 1)
                carry(pool, T.pool_passed)
                nc.gpsimd.tensor_tensor(nb2[:, group(g)], nm2[g.slot][:, :], rs2[:, group(g)], ALU.mult
                                        ).then_inc(T.nb2_ready, 1)

            def to_lists(g, by_batch=False):
                pool.wait_ge(T.stage_free, g.n + 1)
                carry(pool, T.pool_passed)
                nc.gpsimd.tensor_copy(stage[g.slot].bitcast(I32)[:, :].rearrange("p (g c) -> p g c", g=G)[:, :, 2 * D],
                                      numbers[:, group(g)]).then_inc(T.id_staged, 1)
                pool.wait_ge(T.id_staged, g.n + 1)
                pool.wait_ge(T.n2_staged, g.n + 1)
                pool.wait_ge(T.pos_ready, g.n + 1)
                if not by_batch:
                    pool.wait_ge(T.acc_ready, g.n + 1)
                carry(pool, T.pool_passed)
                for j in range(G):
                    if by_batch:
                        pool.wait_ge(T.batch_acc, j + 1)
                    nc.gpsimd.indirect_dma_start(
                        rows, bass.IndirectOffsetOnAxis(ap=pos[g.slot][:, j:j + 1], axis=0),
                        stage[g.slot][:, j * ROW:(j + 1) * ROW], None, bounds_check=E * PAD_TILES * R - 1,
                        oob_is_err=False).then_inc(listed[g.slot], 16)

            def give_back(g):
                pool.wait_ge(listed[g.slot], G * 16 * (g.lap + 1))
                pool.sem_inc(T.stage_free, 1)

            def body(g, i):
                if has(i, -4):
                    to_lists(ahead(g, -4))
                if has(i, 0):
                    pool.wait_ge(raw_loaded[g.slot], 16 * (g.lap + 1))
                    split(raw[g.slot][:, :], g.lap * 4 * F + g.slot * 2 * F, T.half_hi, T.half_split, g.n + 1)
                if has(i, 2):
                    rstd1(ahead(g, 2))
                if has(i, -4):
                    give_back(ahead(g, -4))
                if has(i, 0):
                    rstd2(g)

            for g in range(2):
                rstd1(grp(0, g))
            run_groups(pool, body)
            for i in range(NG, NG + 2):
                body(grp(0, i), i)
            to_lists(grp(0, NG - 2))
            to_lists(grp(0, NG - 1), by_batch=True)
            give_back(grp(0, NG - 2))
            give_back(grp(0, NG - 1))
            pool.sem_inc(T.lists_full, 1)

            def slot(t, s):
                if t_has(s, 0):
                    for j in range(2):
                        pool.wait_ge(T.r_out, 2 * t.n + j + 1)
                        carry(pool, T.pool_passed)
                        nc.gpsimd.indirect_dma_start(
                            out_rows, bass.IndirectOffsetOnAxis(ap=row_in[t.slot][:, j, 2 * D:ROW].bitcast(I32), axis=0),
                            row_out[t.slot][:, j * D:(j + 1) * D], None, bounds_check=TOK - 1, oob_is_err=False
                        ).then_inc(scattered[t.slot], 16)

            run_routed(pool, slot)
            for r in range(RING):
                pool.wait_ge(scattered[r], 32 * ((TILES - r + RING - 1) // RING))

        @block.scalar
        def _(act):
            for dst, src in ((wo_s, Wo), (wv_s, Wv), (bcol[:, 0:1], bq.rearrange("(p o) -> p o", o=1)),
                             (bcol[:, 1:2], bv.rearrange("(p o) -> p o", o=1))):
                act.dma_start(dst, src).then_inc(T.folds_loaded, 16)
            act.dma_start(bo_r, bo.rearrange("(o d) -> o d", o=1).to_broadcast([P, D])).then_inc(T.bo_loaded, 16)
            act.wait_ge(T.woT_ps, 1)
            nc.scalar.copy(woT, bank[2][:, 0:P]).then_inc(T.woT_sb, 1)

            def evac_in(g):
                act.wait_ge(T.xnT_ps, g.n + 1)
                if later_than(g, 1):
                    act.wait_ge(T.q_ps, g.n)
                nc.scalar.copy(xnT[:, :], bank[0][:, :]).then_inc(T.xnT_sb, 1)
                act.wait_ge(T.cxT_ps, g.n + 1)
                if later_than(g, 1):
                    act.wait_ge(T.scores_ps, g.n)
                nc.scalar.copy(cxT[:, :], bank[1][:, 0:G * K]).then_inc(T.cxT_sb, 1)

            def gelu(g, k, pair=2):
                act.wait_ge(T.up_ps, NK * g.n + k + 1)
                if k or later_than(g, 1):
                    act.wait_ge(T.inner_ready, NK * g.n + k)
                nc.scalar.activation(sge[:, :], bank[pair][:, :], ACT.Gelu).then_inc(T.gelu_done, 1)

            def queries(g):
                act.wait_ge(T.q_ps, g.n + 1)
                if later_than(g, 1):
                    act.wait_ge(T.scores_ps, g.n)
                nc.scalar.activation(qT[:, :], bank[0][:, :], ACT.Identity, bias=q_bias[:, :]).then_inc(T.q_sb, 1)

            def exponentials(g):
                act.wait_ge(T.nmax_ready, g.n + 1)
                if later_than(g, 1):
                    act.wait_ge(T.prT_ps, g.n)
                for j in range(G):
                    last = nc.scalar.activation(pr[:, j * K:(j + 1) * K], bank[4][:, j * K:(j + 1) * K],
                                                ACT.Exp, bias=nmx[:, j:j + 1], scale=SCALE,
                                                accum_out=sm[:, j:j + 1])
                last.then_inc(T.exp_done, 1)

            def copy_n2T(g):
                act.wait_ge(T.n2T_ps, g.n + 1)
                if later_than(g, 1):
                    act.wait_ge(T.logits_ps, g.n)
                    act.wait_ge(T.hilo_ready, g.n)
                nc.scalar.copy(n2T[:, :], bank[7][:, :]).then_inc(T.n2T_sb, 1)

            def stage_n2(g):
                act.wait_ge(T.nb2_ready, g.n + 1)
                act.wait_ge(T.stage_free, g.n + 1)
                carry(act, T.act_passed)
                for j in range(G):
                    i = bass.ds(g.n * G + j, 1)
                    last = nc.scalar.activation(stage[g.slot][:, j * ROW + D:j * ROW + 2 * D], batch(g, j),
                                                ACT.Identity, bias=nb2[:, i], scale=rs2[:, i])
                last.then_inc(T.n2_staged, 1)

            def body(g, i):
                c, s, d = ahead(g, -1), ahead(g, -2), ahead(g, -3)
                if has(i, -2):
                    gelu(s, 0)
                if has(i, 0):
                    queries(g)
                if has(i, -3):
                    stage_n2(d)
                if has(i, -2):
                    gelu(s, 1)
                if has(i, -1):
                    copy_n2T(c)
                if has(i, -2):
                    gelu(s, 2)
                if has(i, 0):
                    exponentials(g)
                if has(i, 1):
                    evac_in(ahead(g, 1))
                if has(i, -2):
                    gelu(s, 3)
                if has(i, 0):
                    act.wait_ge(T.prT_ps, g.n + 1)
                    if later_than(g, 1):
                        act.wait_ge(T.att_ps, g.n)
                    nc.scalar.copy(prT[0:K, :], bank[4][0:K, :]).then_inc(T.prT_sb, 1)

            evac_in(grp(0, 0))
            run_groups(act, body)
            before, end = grp(0, NG - 2), grp(0, NG - 1)
            gelu(before, 0)
            stage_n2(grp(0, NG - 3))
            gelu(before, 1, pair=0)
            copy_n2T(end)
            gelu(before, 2)
            gelu(before, 3, pair=0)
            gelu(end, 0)
            stage_n2(before)
            for k in range(1, NK):
                gelu(end, k, pair=0 if k % 2 else 2)
            stage_n2(end)

            def copy_w12(t, w, e):
                if w == 0 and later_than(t, 2):
                    act.wait_ge(T.r_up_ps, 2 * (t.n - 1))
                    carry(act, T.act_passed)
                nc.scalar.copy(w12_t[t.slot % 2][:, w * 2 * F:(w + 1) * 2 * F],
                               w12[:, bass.ds(e * (4 * F) + w * 2 * F, 2 * F)].bitcast(F32)
                               ).then_inc(T.w12_copied, 1)

            def r_gelu(t, half):
                act.wait_ge(T.r_up_ps, 2 * t.n + half + 1)
                if later_than(t, 1):
                    act.wait_ge(T.r_inner, 2 * t.n - 1 + half)
                nc.scalar.activation(ge[half], bank[2 * half][:, :], ACT.Gelu).then_inc(T.r_gelu, 1)

            def load_expert(t):
                return act.value_load(te[0:1, bass.ds(t.n, 1)], min_val=0, max_val=E - 1)

            def slot(t, s):
                if t_has(s, 2):
                    f = t_ahead(t, 2)
                    e = load_expert(f)
                for half in range(2):
                    if t_has(s, 2):
                        copy_w12(f, half, e)
                    if t_has(s, 1):
                        r_gelu(t_ahead(t, 1), half)

            act.wait_ge(T.tiles_ready, 1)
            act.wait_ge(T.half_split, NG)
            act.wait_ge(T.inner_ready, NK * NG)
            e = load_expert(tile(0, 0))
            for w in range(2):
                copy_w12(tile(0, 0), w, e)
            run_routed(act, slot)

        @block.vector
        def _(dve):
            def norm_stats(src, st, mv, g, stats, ready):
                for j in range(G):
                    last = nc.vector.bn_stats(st[g.slot][:, j, :], src(j))
                last.then_inc(stats, 1)
                dve.wait_ge(stats, g.n + 1)
                carry(dve, T.dve_passed)
                for j in range(G):
                    last = nc.vector.bn_aggr(mv[g.slot][:, j, :], st[g.slot][:, j, :])
                last.then_inc(ready, 1)

            def stats1(g):
                dve.wait_ge(in_loaded[g.slot], 32 * (g.lap + 1))
                if later_than(g, 2):
                    dve.wait_ge(T.rstd1, g.n - 1)
                carry(dve, T.dve_passed)
                norm_stats(lambda j: batch(g, j), st1, mv1, g, T.stats1, T.mv1_ready)

            def normalise(dst, mv, rs, g, ready):
                for j in range(G):
                    last = nc.vector.tensor_scalar(b4(dst)[:, j, :], batch(g, j), mv[g.slot][:, j, 0:1], rs(j),
                                                   ALU.subtract, ALU.mult)
                last.then_inc(ready, 1)

            def norm1(g):
                dve.wait_ge(T.rstd1, g.n + 1)
                if later_than(g, 1):
                    dve.wait_ge(T.xnT_ps, g.n)
                normalise(xn[:, :], mv1, lambda j: rs1[g.slot][:, j:j + 1], g, T.xn_ready)

            def norm2(g):
                dve.wait_ge(T.rstd2, g.n + 1)
                if later_than(g, 2):
                    dve.wait_ge(T.n2T_ps, g.n - 1)
                normalise(n2[g.slot][:, :], mv2, lambda j: rs2[:, bass.ds(g.n * G + j, 1)], g, T.n2_ready)

            def values(g):
                dve.wait_ge(T.v_ps, g.n + 1)
                if later_than(g, 1):
                    dve.wait_ge(T.att_ps, g.n)
                nc.vector.tensor_tensor(b4(vb[:, :])[0:K], b4(bank[1][:, :])[0:K],
                                        bb[0:K, :].unsqueeze(1).to_broadcast([K, G, D]), ALU.add
                                        ).then_inc(T.v_sb, 1)

            def maxima(g):
                dve.wait_ge(T.scores_ps, g.n + 1)
                nc.vector.reduce_max(mx0[:, :], bank[4][:, 0:G * K].rearrange("p (g k) -> p g k", g=G),
                                     AX.X).then_inc(T.max_ready, 1)
                if later_than(g, 1):
                    dve.wait_ge(T.exp_done, g.n)
                dve.wait_ge(T.max_ready, g.n + 1)
                nc.vector.tensor_scalar(nmx[:, :], mx0[:, :], -SCALE, None, ALU.mult
                                        ).then_inc(T.nmax_ready, 1)

            def probabilities(g):
                dve.wait_ge(T.exp_done, g.n + 1)
                nc.vector.reciprocal(rsm[:, :], sm[:, :]).then_inc(T.rsum_ready, 1)
                dve.wait_ge(T.rsum_ready, g.n + 1)
                pv = pr[:, :].rearrange("p (g k) -> p g k", g=G)
                nc.vector.tensor_tensor(pv, pv, rsm[:, :].unsqueeze(2).to_broadcast([P, G, K]), ALU.mult
                                        ).then_inc(T.probs_ready, 1)

            def residual(g):
                dve.wait_ge(T.att_ps, g.n + 1)
                nc.vector.tensor_tensor(res[:, group(g), :], res[:, group(g), :], b4(bank[7][:, :]), ALU.add
                                        ).then_inc(T.res_ready, 1)
                dve.wait_ge(T.res_ready, g.n + 1)
                if later_than(g, 2):
                    dve.wait_ge(T.rstd2, g.n - 1)
                carry(dve, T.dve_passed)
                norm_stats(lambda j: batch(g, j), st2, mv2, g, T.stats2, T.mv2_ready)

            def hilo(g):
                dve.wait_ge(T.n2T_sb, g.n + 1)
                if later_than(g, 2):
                    dve.wait_ge(T.up_ps, NK * (g.n - 1))
                nc.vector.tensor_copy(shi[g.slot][:, :], n2T[:, :]).then_inc(T.hilo_hi, 1)
                dve.wait_ge(T.hilo_hi, g.n + 3)
                nc.vector.tensor_tensor(slo[g.slot][:, :], n2T[:, :], shi[g.slot][:, :].bitcast(F32), ALU.subtract
                                        ).then_inc(T.hilo_ready, 1)

            def choose(g):
                dve.wait_ge(T.logits_ps, g.n + 1)
                lg = bank[7][:, 0:G * E].rearrange("p (g e) -> p g e", g=G)
                nc.vector.reduce_max(best[:, :], lg, AX.X).then_inc(T.choice, 1)
                dve.wait_ge(T.choice, 4 * g.n + 1)
                nc.vector.tensor_tensor(is_best[:, :, :], lg, best[:, :].unsqueeze(2).to_broadcast([P, G, E]),
                                        ALU.is_equal).then_inc(T.choice, 1)
                dve.wait_ge(T.choice, 4 * g.n + 2)
                dve.sem_inc(T.logits_read, 1)
                nc.vector.tensor_tensor(is_best[:, :, :], is_best[:, :, :],
                                        weight[:, :].unsqueeze(1).to_broadcast([P, G, E]), ALU.mult
                                        ).then_inc(T.choice, 1)
                dve.wait_ge(T.choice, 4 * g.n + 3)
                nc.vector.reduce_max(win[:, :], is_best[:, :, :], AX.X).then_inc(T.choice, 1)
                if later_than(g, 2):
                    dve.wait_ge(T.counted, g.n - 1)
                dve.wait_ge(T.choice, 4 * g.n + 4)
                nc.vector.tensor_tensor(oh[g.slot][:, :, :], is_best[:, :, :],
                                        win[:, :].unsqueeze(2).to_broadcast([P, G, E]), ALU.is_equal
                                        ).then_inc(T.onehot, 1)

            def positions(g):
                dve.wait_ge(T.ranks_ps, g.n + 1)
                nc.vector.tensor_tensor(at_row[:, :, :], bank[5][:, 0:G * E].rearrange("p (g e) -> p g e", g=G),
                                        oh[g.slot][:, :, :], ALU.mult).then_inc(T.ranks_read, 1)
                dve.wait_ge(T.ranks_read, g.n + 1)
                nc.vector.tensor_reduce(pos_f[:, :], at_row[:, :, :], AX.X, ALU.add).then_inc(T.pos_summed, 1)

            def store_positions(g):
                dve.wait_ge(T.stage_free, g.n + 1)
                dve.wait_ge(T.pos_summed, g.n + 1)
                nc.vector.tensor_copy(pos[g.slot][:, :], pos_f[:, :]).then_inc(T.pos_ready, 1)

            def inner(g, k, pair=2):
                dve.wait_ge(T.gelu_done, NK * g.n + k + 1)
                if k == 0 and later_than(g, 2):
                    dve.wait_ge(T.down_ps, g.n - 1)
                nc.vector.tensor_tensor(sg[g.slot][:, k * 512:(k + 1) * 512], sge[:, :], bank[pair + 1][:, :], ALU.mult
                                        ).then_inc(T.inner_ready, 1)

            def accumulate(g):
                dve.wait_ge(T.down_ps, g.n + 1)
                dve.wait_ge(T.stage_free, g.n + 1)
                nc.vector.tensor_tensor(stage[g.slot][:, :].rearrange("p (g c) -> p g c", g=G)[:, :, 0:D],
                                        res[:, group(g), :], b4(bank[6][:, :]), ALU.add
                                        ).then_inc(T.acc_ready, 1)

            def accumulate_batch(g, j):
                dve.wait_ge(T.batch_down_ps, j + 1)
                if j == 0:
                    dve.wait_ge(T.stage_free, g.n + 1)
                nc.vector.tensor_tensor(stage[g.slot][:, j * ROW:j * ROW + D], batch(g, j),
                                        bank[LAST_BANKS[j]][:, 0:D], ALU.add).then_inc(T.batch_acc, 1)

            def body(g, i):
                c, s, d = ahead(g, -1), ahead(g, -2), ahead(g, -3)
                if has(i, -2):
                    inner(s, 0)
                if has(i, 0):
                    values(g)
                if has(i, -1):
                    norm2(c)
                if has(i, -2):
                    inner(s, 1)
                if has(i, 0):
                    maxima(g)
                if has(i, 1):
                    norm1(ahead(g, 1))
                if has(i, -3):
                    positions(d)
                    store_positions(d)
                if has(i, -2):
                    inner(s, 2)
                if has(i, -1):
                    hilo(c)
                if has(i, 2):
                    stats1(ahead(g, 2))
                if has(i, 0):
                    probabilities(g)
                if has(i, -1):
                    choose(c)
                if has(i, -2):
                    inner(s, 3)
                if has(i, -3):
                    accumulate(d)
                if has(i, 0):
                    residual(g)

            stats1(grp(0, 0))
            dve.wait_ge(T.folds_loaded, 6 * 16)
            nc.vector.tensor_copy(bq_r, bcol[:, 0:1].to_broadcast([P, P])).then_inc(T.dve_consts, 1)
            nc.vector.tensor_copy(bv_r, bcol[:, 1:2].to_broadcast([P, P])).then_inc(T.dve_consts, 1)
            norm1(grp(0, 0))
            dve.wait_ge(T.fold_ps, 1)
            nc.vector.tensor_copy(fold_q[:, :], bank[3][:, 0:P]).then_inc(T.fold_sb, 1)
            nc.vector.tensor_copy(q_bias[:, :], bank[3][:, P:P + 1]).then_inc(T.fold_sb, 1)
            dve.wait_ge(T.fold_ps, 2)
            nc.vector.tensor_copy(fold_v[:, :], bank[4][:, 0:P]).then_inc(T.fold_sb, 1)
            dve.wait_ge(T.bo_loaded, 16)
            nc.vector.tensor_tensor(bb[:, :], bank[4][:, P:2 * P], bo_r, ALU.add).then_inc(T.fold_sb, 1)
            stats1(grp(0, 1))
            dve.wait_ge(T.wshared_loaded, 32)
            for w in range(2):
                base = E * 4 * F + w * 2 * F
                nc.vector.tensor_copy(w12[:, base:base + F], ws_raw[:, w * F:(w + 1) * F]).then_inc(T.hilo_hi, 1)
            dve.wait_ge(T.hilo_hi, 2)
            for w in range(2):
                base = E * 4 * F + w * 2 * F
                nc.vector.tensor_tensor(w12[:, base + F:base + 2 * F], ws_raw[:, w * F:(w + 1) * F],
                                        w12[:, base:base + F].bitcast(F32), ALU.subtract).then_inc(T.dve_consts, 1)
            run_groups(dve, body)

            last3, before, end = grp(0, NG - 3), grp(0, NG - 2), grp(0, NG - 1)
            inner(before, 0)
            norm2(end)
            inner(before, 1, pair=0)
            positions(last3)
            store_positions(last3)
            hilo(end)
            choose(end)
            inner(before, 2)
            positions(before)
            store_positions(before)
            accumulate(last3)
            inner(before, 3, pair=0)
            positions(end)
            inner(end, 0)

            links = [4 * NG]

            def link(ins):
                links[0] += 1
                ins.then_inc(T.choice, 1)
                dve.wait_ge(T.choice, links[0])

            accumulate(before)
            dve.wait_ge(T.counted, NG)
            ranks = bank[5][0:1, 0:E]
            link(nc.vector.tensor_copy(pad_i[:, :], ranks))
            dve.sem_inc(T.pads_ready, 1)
            inner(end, 1, pair=0)
            store_positions(end)
            link(nc.vector.tensor_tensor(cnt[:, :], ranks, start_e[0:1, :], ALU.subtract))
            link(nc.vector.tensor_scalar(cnt_i[:, :], cnt[:, :], float(R - 1), None, ALU.add))
            link(nc.vector.tensor_single_scalar(cnt_i[:, :], cnt_i[:, :], int(np.log2(R)), ALU.arith_shift_right))
            inner(end, 2)
            link(nc.vector.tensor_copy(cnt[:, :], cnt_i[:, :]))
            link(nc.vector.tensor_tensor_scan(tend[:, :], ones_f[0:1, :].to_broadcast([1, E]), cnt[:, :], 0.0,
                                              ALU.mult, ALU.add))
            link(nc.vector.tensor_scalar(spare[:, :], cnt[:, :], -1.0, float(PAD_TILES), ALU.mult, ALU.add))
            inner(end, 3, pair=0)
            accumulate_batch(end, 0)
            link(nc.vector.tensor_tensor(tcmp, iota_t[:, :].unsqueeze(2).to_broadcast([1, TILES, E]),
                                         tend[:, :].unsqueeze(1).to_broadcast([1, TILES, E]), ALU.is_ge))
            link(nc.vector.tensor_tensor(tskip, tcmp, spare[:, :].unsqueeze(1).to_broadcast([1, TILES, E]), ALU.mult))
            accumulate_batch(end, 1)
            link(nc.vector.tensor_reduce(to_f[:, :], tskip, AX.X, ALU.add))
            accumulate_batch(end, 2)
            link(nc.vector.tensor_tensor(to_f[:, :], to_f[:, :], iota_t[:, :], ALU.add))
            link(nc.vector.tensor_scalar(to[:, :], to_f[:, :], float(E * PAD_TILES), float(R), ALU.min, ALU.mult))
            accumulate_batch(end, 3)
            link(nc.vector.tensor_reduce(te_f[:, :], tcmp, AX.X, ALU.add))
            link(nc.vector.tensor_scalar(te[:, :], te_f[:, :], float(E - 1), None, ALU.min))
            dve.sem_inc(T.tiles_ready, 1)

            def copy_w3(t):
                e = dve.value_load(te[0:1, bass.ds(t.n, 1)], min_val=0, max_val=E - 1)
                if later_than(t, 2):
                    dve.wait_ge(T.r_down_ps, 2 * (t.n - 1))
                    carry(dve, T.dve_passed)
                nc.vector.tensor_copy(w3_t[t.slot % 2], w3[:, bass.ds(e * F, F)]).then_inc(T.w3_copied, 1)

            def r_inner(t, half):
                dve.wait_ge(T.r_gelu, 2 * t.n + half + 1)
                if half == 0 and later_than(t, 2):
                    dve.wait_ge(T.r_down_ps, 2 * (t.n - 1))
                nc.vector.tensor_tensor(gg[t.slot % 2][:, half * F:(half + 1) * F], ge[half],
                                        bank[2 * half + 1][:, :], ALU.mult).then_inc(T.r_inner, 1)

            def r_out(t, j):
                dve.wait_ge(T.r_down_ps, 2 * t.n + j + 1)
                if j == 0 and later_than(t, RING):
                    dve.wait_ge(scattered[t.slot], 32 * t.lap)
                nc.vector.tensor_tensor(row_out[t.slot][:, j * D:(j + 1) * D], row_in[t.slot][:, j, 0:D],
                                        bank[5 + j][:, 0:D], ALU.add).then_inc(T.r_out, 1)

            def slot(t, s):
                if t_has(s, 2):
                    parts(t_ahead(t, 2))
                if t_has(s, 1):
                    copy_w3(t_ahead(t, 1))
                for half in range(2):
                    if t_has(s, 1):
                        r_inner(t_ahead(t, 1), half)
                    if t_has(s, 0):
                        r_out(t, half)

            def parts(t):
                dve.wait_ge(T.xT_ps, t.n + 1)
                if later_than(t, 2):
                    dve.wait_ge(T.r_up_ps, 2 * (t.n - 1))
                src = bank[T_BANKS[t.slot % 2]][:, 0:R]
                nc.vector.tensor_copy(xh[t.slot % 2][:, :], src).then_inc(T.x_hi, 1)
                dve.wait_ge(T.x_hi, t.n + 1)
                nc.vector.tensor_tensor(xl[t.slot % 2][:, :], src, xh[t.slot % 2][:, :].bitcast(F32), ALU.subtract
                                        ).then_inc(T.x_ready, 1)

            dve.wait_ge(T.w3_loaded, 16)
            dve.wait_ge(T.n2_staged, NG)
            parts(tile(0, 0))
            run_routed(dve, slot)

        @block.tensor
        def _(pe):
            mm, tr = nc.tensor.matmul, nc.tensor.transpose
            pe.wait_ge(T.consts, 3)
            pe.wait_ge(T.folds_loaded, 6 * 16)
            tr(bank[2][:, 0:P], wo_s, ident[:, :]).then_inc(T.woT_ps, 1)
            pe.wait_ge(T.dve_consts, 2)
            mm(bank[3][:, 0:P], wq_s, wk_s, start=True, stop=True)
            mm(bank[3][:, P:2 * P], wk_s, bq_r, start=True, stop=True).then_inc(T.fold_ps, 1)
            pe.wait_ge(T.woT_sb, 1)
            mm(bank[4][:, 0:P], wv_s, woT, start=True, stop=True)
            mm(bank[4][:, P:2 * P], bv_r, woT, start=True, stop=True).then_inc(T.fold_ps, 1)

            def transpose_in(g):
                pe.wait_ge(T.xn_ready, g.n + 1)
                if later_than(g, 1):
                    pe.wait_ge(T.q_sb, g.n)
                for j in range(G):
                    last = tr(bank[0][:, j * P:(j + 1) * P], b4(xn[:, :])[:, j, :], ident[:, :])
                last.then_inc(T.xnT_ps, 1)
                pe.wait_ge(in_loaded[g.slot], 32 * (g.lap + 1))
                if later_than(g, 1):
                    pe.wait_ge(T.v_sb, g.n)
                for j in range(G):
                    last = tr(bank[1][:, j * K:(j + 1) * K], b4(cx[g.slot][:, :])[0:K, j, :], ident[0:K, 0:K])
                last.then_inc(T.cxT_ps, 1)

            def project(g):
                pe.wait_ge(T.xnT_sb, g.n + 1)
                mm(bank[0][:, :], fold_q[:, :], xnT[:, :], start=True, stop=True).then_inc(T.q_ps, 1)
                pe.wait_ge(T.cxT_sb, g.n + 1)
                for j in range(G):
                    last = mm(bank[1][0:K, j * D:(j + 1) * D], cxT[:, j * K:(j + 1) * K], fold_v[:, :],
                              start=True, stop=True)
                last.then_inc(T.v_ps, 1)

            def scores(g):
                pe.wait_ge(T.q_sb, g.n + 1)
                if later_than(g, 1):
                    pe.wait_ge(T.prT_sb, g.n)
                for j in range(G):
                    last = mm(bank[4][:, j * K:(j + 1) * K], qT[:, j * P:(j + 1) * P],
                              cxT[:, j * K:(j + 1) * K], start=True, stop=True)
                last.then_inc(T.scores_ps, 1)

            def transpose_probs(g):
                pe.wait_ge(T.probs_ready, g.n + 1)
                for j in range(G):
                    last = tr(bank[4][0:K, j * P:(j + 1) * P], pr[:, j * K:(j + 1) * K], ident[:, :])
                last.then_inc(T.prT_ps, 1)

            def attend(g):
                pe.wait_ge(T.prT_sb, g.n + 1)
                pe.wait_ge(T.v_sb, g.n + 1)
                if later_than(g, 1):
                    pe.wait_ge(T.logits_read, g.n)
                for j in range(G):
                    last = mm(bank[7][:, j * D:(j + 1) * D], prT[0:K, j * P:(j + 1) * P],
                              vb[0:K, j * D:(j + 1) * D], start=True, stop=True)
                last.then_inc(T.att_ps, 1)

            def transpose_n2(g):
                pe.wait_ge(T.n2_ready, g.n + 1)
                for j in range(G):
                    last = tr(bank[7][:, j * P:(j + 1) * P], n2[g.slot][:, j * D:(j + 1) * D], ident[:, :])
                last.then_inc(T.n2T_ps, 1)

            def logits(g):
                if not later_than(g, 1):
                    pe.wait_ge(T.wg_loaded, 16)
                pe.wait_ge(T.n2T_sb, g.n + 1)
                for j in range(G):
                    last = mm(bank[7][:, j * E:(j + 1) * E], n2T[:, j * P:(j + 1) * P], wg[:, :],
                              start=True, stop=True)
                last.then_inc(T.logits_ps, 1)

            def up(g, k, pair=2, pairs=1):
                if k == 0:
                    if not later_than(g, 1):
                        pe.wait_ge(T.dve_consts, 4)
                        pe.wait_ge(T.w3s_loaded, 16)
                    pe.wait_ge(T.hilo_ready, g.n + 1)
                if k or later_than(g, 1):
                    pe.wait_ge(T.inner_ready, NK * g.n + k + 1 - pairs)
                for w in range(2):
                    base = E * 4 * F + w * 2 * F + k * P
                    hi, lo = w12[:, base:base + P], w12[:, base + F:base + F + P]
                    dst = bank[pair + w][:, :]
                    mm(dst, hi, shi[g.slot][:, :], start=True, stop=False)
                    mm(dst, hi, slo[g.slot][:, :], start=False, stop=False)
                    last = mm(dst, lo, shi[g.slot][:, :], start=False, stop=True)
                last.then_inc(T.up_ps, 1)

            def down(g, half):
                if half == 0:
                    pe.wait_ge(T.inner_ready, NK * (g.n + 1))
                    if later_than(g, 1):
                        pe.wait_ge(T.acc_ready, g.n)
                for j in range(2 * half, 2 * half + 2):
                    for k in range(NK):
                        last = mm(bank[6][:, j * D:(j + 1) * D], sg[g.slot][:, k * 512 + j * P:k * 512 + (j + 1) * P],
                                  w3[:, (E * NK + k) * D:(E * NK + k + 1) * D], start=k == 0, stop=k == NK - 1)
                if half:
                    last.then_inc(T.down_ps, 1)

            def down_batch(g, j, slices):
                for k in slices:
                    last = mm(bank[LAST_BANKS[j]][:, 0:D], sg[g.slot][:, k * 512 + j * P:k * 512 + (j + 1) * P],
                              w3[:, (E * NK + k) * D:(E * NK + k + 1) * D], start=k == 0, stop=k == NK - 1)
                if k == NK - 1:
                    last.then_inc(T.batch_down_ps, 1)

            def count(first, batches, lhsT, rhs):
                return mm(bank[5][:, first * E:(first + batches) * E], lhsT, rhs,
                          start=False, stop=True, skip_group_check=True)

            def rank(g):
                pe.wait_ge(T.onehot, g.n + 1)
                all_oh = oh[g.slot][:, :, :].rearrange("p g e -> p (g e)")
                last = count(0, G, tri[:, :], all_oh)
                for j in range(G - 1):
                    last = count(j + 1, G - 1 - j, ones_b[:, :],
                                 oh[g.slot][:, j:j + 1, :].to_broadcast([P, G - 1 - j, E]))
                last.then_inc(T.ranks_ps, 1)

            def finish_count(g):
                pe.wait_ge(T.ranks_read, g.n + 1)
                all_oh = oh[g.slot][:, :, :].rearrange("p g e -> p (g e)")
                last = count(0, G, rest[:, :], all_oh)
                for j in range(1, G):
                    last = count(0, j, ones_b[:, :], oh[g.slot][:, j:j + 1, :].to_broadcast([P, j, E]))
                last.then_inc(T.counted, 1)

            def body(g, i):
                c, s, d = ahead(g, -1), ahead(g, -2), ahead(g, -3)
                if has(i, -2):
                    up(s, 0)
                if has(i, 0):
                    project(g)
                if has(i, -2):
                    up(s, 1)
                if has(i, 0):
                    scores(g)
                if has(i, -1):
                    transpose_n2(c)
                if has(i, -3):
                    rank(d)
                if has(i, -2):
                    up(s, 2)
                if has(i, -3):
                    down(d, 0)
                if has(i, 1):
                    transpose_in(ahead(g, 1))
                if has(i, -2):
                    up(s, 3)
                if has(i, -3):
                    finish_count(d)
                if has(i, -1):
                    logits(c)
                if has(i, 0):
                    transpose_probs(g)
                if has(i, -3):
                    down(d, 1)
                if has(i, 0):
                    attend(g)

            transpose_in(grp(0, 0))
            mm(bank[5][:, 0:G * E], ones_b[:, :], start_b[:, :, :].rearrange("p g e -> p (g e)"), start=True, stop=True,
               skip_group_check=True)
            pe.wait_ge(T.fold_sb, 4)
            run_groups(pe, body)

            last3, before, end = grp(0, NG - 3), grp(0, NG - 2), grp(0, NG - 1)
            up(before, 0)
            up(before, 1, pair=0, pairs=2)
            rank(last3)
            down(last3, 0)
            transpose_n2(end)
            finish_count(last3)
            rank(before)
            logits(end)
            up(before, 2, pairs=2)
            down(last3, 1)
            up(before, 3, pair=0, pairs=2)
            finish_count(before)
            rank(end)
            up(end, 0, pairs=2)
            down(before, 0)
            down(before, 1)
            finish_count(end)
            up(end, 1, pair=0, pairs=2)
            up(end, 2, pairs=2)
            up(end, 3, pair=0, pairs=2)
            pe.wait_ge(T.inner_ready, NK * NG - 1)
            pe.wait_ge(T.acc_ready, NG - 1)
            pe.wait_ge(T.logits_read, NG)
            for j in range(2):
                down_batch(end, j, range(NK - 1))
            pe.wait_ge(T.inner_ready, NK * NG)
            for j in range(G):
                down_batch(end, j, (NK - 1,) if j < 2 else range(NK))

            def fetch_T(t):
                pe.wait_ge(tile_loaded[t.slot], 16 * (t.lap + 1))
                for j in range(2):
                    last = tr(bank[T_BANKS[t.slot % 2]][:, j * P:(j + 1) * P], row_in[t.slot][:, j, D:2 * D], ident[:, :])
                last.then_inc(T.xT_ps, 1)

            def r_up(t, half):
                q = t.slot % 2
                if half == 0:
                    pe.wait_ge(T.w12_copied, 2 * (t.n + 1))
                if later_than(t, 1):
                    pe.wait_ge(T.r_inner, 2 * t.n - 1 + half)
                for w in range(2):
                    for k in (2 * half, 2 * half + 1):
                        base = w * 2 * F + k * P
                        hi, lo = w12_t[q][:, base:base + P], w12_t[q][:, base + F:base + F + P]
                        dst = bank[2 * half + w][:, k % 2 * R:(k % 2 + 1) * R]
                        mm(dst, hi, xh[q][:, :], start=True, stop=False)
                        mm(dst, hi, xl[q][:, :], start=False, stop=False)
                        last = mm(dst, lo, xh[q][:, :], start=False, stop=True)
                last.then_inc(T.r_up_ps, 1)

            def r_down(t, j):
                if j == 0:
                    pe.wait_ge(T.r_inner, 2 * (t.n + 1))
                    pe.wait_ge(T.w3_copied, t.n + 1)
                if later_than(t, 1):
                    pe.wait_ge(T.r_out, 2 * t.n - 1 + j)
                for k in range(NK):
                    last = mm(bank[5 + j][:, 0:D], gg[t.slot % 2][:, k * R + j * P:k * R + (j + 1) * P],
                              w3_t[t.slot % 2][:, k * D:(k + 1) * D], start=k == 0, stop=k == NK - 1)
                last.then_inc(T.r_down_ps, 1)

            def slot(t, s):
                if t_has(s, 2):
                    fetch_T(t_ahead(t, 2))
                if t_has(s, 1):
                    pe.wait_ge(T.x_ready, t.n + 2)
                for half in range(2):
                    if t_has(s, 1):
                        r_up(t_ahead(t, 1), half)
                    if t_has(s, 0):
                        r_down(t, half)

            fetch_T(tile(0, 0))
            run_routed(pe, slot)


_INS = ['x', 'ctx_1024', 'L0_xattn_Wk', 'L0_xattn_Wv', 'L0_xattn_bv', 'L0_xattn_Wq', 'L0_xattn_bq', 'L0_xattn_Wo',
        'L0_xattn_bo', 'L0_ffn_w1s', 'L0_ffn_w2s', 'L0_ffn_w3s', 'L0_ffn_W1', 'L0_ffn_W2', 'L0_ffn_W3', 'L0_ffn_Wg']


def kernel(**inputs):
    import concourse.bacc as bacc
    from concourse.bass_utils import run_bass_kernel_spmd

    nc = bacc.Bacc("TRN2", target_bir_lowering=False, num_devices=1)
    arrays, args = {}, []
    for name in _INS:
        a = np.ascontiguousarray(inputs[name])
        arrays[name] = a
        args.append(nc.dram_tensor(name, a.shape, mybir.dt.from_np(a.dtype), kind="ExternalInput").ap())
    args.append(nc.dram_tensor("y", (B, P, D), F32, kind="ExternalOutput").ap())
    xattn_moe(nc, *args)
    r = run_bass_kernel_spmd(nc, [arrays], core_ids=[0])
    return r.results[0]["y"]
```
